# Optimizing a Trainium2 kernel written in Bass

```python
import numpy as np
import jax
import jax.numpy as jnp

def _softmax(x, axis=-1):
    return jax.nn.softmax(x, axis=axis)

def _gelu(x):
    return jax.nn.gelu(x, approximate=True)

def _silu(x):
    return jax.nn.silu(x)

def _sigmoid(x):
    return jax.nn.sigmoid(x)

def _layernorm(x, axis=-1, eps=1e-05):
    m = jnp.mean(x, axis=axis, keepdims=True)
    v = jnp.var(x, axis=axis, keepdims=True)
    return (x - m) / jnp.sqrt(v + eps)

def _scatter_add(tgt, idx, src, axis=0):
    return tgt.at[idx].add(src)

def _segment_sum(src, seg, n):
    return jax.ops.segment_sum(src, seg, n)
kernel_name = 'mk_xattn_seq_d4_seqx_r8_3917e2'

def setup_inputs(seed: int=0):
    np.random.seed(seed)
    _w = jnp.asarray

    def _rec_inputs():
        import jax
        import jax.numpy as jnp
        _rk = jax.random.key(seed)
        x = -0.000125 + 0.9999 * jax.random.normal(jax.random.fold_in(_rk, 1), (2, 512, 128), jnp.float32)
        _lenS = 512 - jax.random.randint(jax.random.fold_in(_rk, 7), (2,), 0, max(1, 512 // 4) + 1, jnp.int32)
        _lenS2 = 77 - jax.random.randint(jax.random.fold_in(_rk, 8), (2,), 0, max(1, 77 // 4) + 1, jnp.int32)
        _ctx_512P = jax.random.normal(jax.random.fold_in(_rk, 11), (2, 16, 64), jnp.float32)
        _ctx_512c = jax.random.dirichlet(jax.random.fold_in(_rk, 511), 0.3 * jnp.ones((16,), jnp.float32), (2, 77))
        _ctx_512t = jnp.einsum('bsk,bkd->bsd', _ctx_512c, _ctx_512P)
        _ctx_512t = _ctx_512t * jax.lax.rsqrt(jnp.mean(jnp.square(_ctx_512t)) + 1e-12) * 0.953939
        ctx_512 = 0.000227908 + 0.99994 * (_ctx_512t + 0.3 * jax.random.normal(jax.random.fold_in(_rk, 611), (2, 77, 64), jnp.float32))
        _validS = jnp.arange(512)[None, :] < _lenS[:, None]
        _validS2 = jnp.arange(77)[None, :] < _lenS2[:, None]
        _causal = jnp.tril(jnp.ones((512, 512), dtype=bool))
        mask_BxSxS_ik0 = jnp.where(jnp.broadcast_to(_validS[:, None, :], (2, 512, 512)), 0, 1).astype(jnp.int32)
        mask_Bx1xS2_if1 = jnp.where(jnp.ones((2, 1, 77), dtype=bool), 1, 0).astype(jnp.int32)
        return (x, ctx_512, mask_BxSxS_ik0, mask_Bx1xS2_if1)
    x, ctx_512, mask_BxSxS_ik0, mask_Bx1xS2_if1 = _rec_inputs()

    def _L0_xattn_setup():
        import jax, jax.numpy as jnp
        import numpy as np
        B, T, E = (8, 512, 128)
        M, L = (32, 64)
        EPS = 1e-06
        key = jax.random.key(seed)
        ks = jax.random.split(key, 5)
        return {'emb': jax.random.normal(ks[0], (B, T, E), dtype=jnp.float32), 'latent': jax.random.normal(ks[1], (B, M, L), dtype=jnp.float32), 'Wq': jax.random.normal(ks[2], (E, E), dtype=jnp.float32) * (1.0 / np.sqrt(E)), 'bq': jnp.zeros((E,), dtype=jnp.float32), 'Wk': jax.random.normal(ks[3], (L, E), dtype=jnp.float32) * (1.0 / np.sqrt(L)), 'bk': jnp.zeros((E,), dtype=jnp.float32), 'Wv': jax.random.normal(ks[4], (L, E), dtype=jnp.float32) * (1.0 / np.sqrt(L)), 'bv': jnp.zeros((E,), dtype=jnp.float32), 'gamma': jnp.ones((E,), dtype=jnp.float32), 'beta': jnp.zeros((E,), dtype=jnp.float32)}
    _L0_xattn_all = _L0_xattn_setup()
    _L0_xattn_in = {k: v for k, v in _L0_xattn_all.items() if k in ('Wq', 'bq', 'Wk', 'bk', 'Wv', 'bv', 'gamma', 'beta')}
    del _L0_xattn_all

    def _L1_xattn_setup():
        import jax, jax.numpy as jnp
        import numpy as np
        QUERY_DIM = 128
        KEY_DIM = 64
        HIDDEN_DIM = 128
        B, LQ, LK = (8, 256, 256)
        key = jax.random.key(seed)
        ks = jax.random.split(key, 10)
        s_q = 1.0 / np.sqrt(QUERY_DIM)
        s_k = 1.0 / np.sqrt(KEY_DIM)
        s_h = 1.0 / np.sqrt(HIDDEN_DIM)
        return {'query': jax.random.normal(ks[0], (B, LQ, QUERY_DIM), jnp.float32), 'key': jax.random.normal(ks[1], (B, LK, KEY_DIM), jnp.float32), 'Wq': jax.random.uniform(ks[2], (QUERY_DIM, HIDDEN_DIM), jnp.float32, -s_q, s_q), 'bq': jax.random.uniform(ks[3], (HIDDEN_DIM,), jnp.float32, -s_q, s_q), 'Wk': jax.random.uniform(ks[4], (KEY_DIM, HIDDEN_DIM), jnp.float32, -s_k, s_k), 'bk': jax.random.uniform(ks[5], (HIDDEN_DIM,), jnp.float32, -s_k, s_k), 'Wv': jax.random.uniform(ks[6], (KEY_DIM, HIDDEN_DIM), jnp.float32, -s_k, s_k), 'bv': jax.random.uniform(ks[7], (HIDDEN_DIM,), jnp.float32, -s_k, s_k), 'Wo': jax.random.uniform(ks[8], (HIDDEN_DIM, QUERY_DIM), jnp.float32, -s_h, s_h), 'bo': jax.random.uniform(ks[9], (QUERY_DIM,), jnp.float32, -s_h, s_h)}
    _L1_xattn_all = _L1_xattn_setup()
    _L1_xattn_in = {k: v for k, v in _L1_xattn_all.items() if k in ('Wq', 'bq', 'Wk', 'bk', 'Wv', 'bv', 'Wo', 'bo')}
    del _L1_xattn_all

    def _L2_xattn_setup():
        import jax, jax.numpy as jnp
        import numpy as np
        B, ST, SS = (8, 64, 72)
        TD, SD = (128, 64)
        L, H, D, FF = (6, 16, 64, 512)

        def _ln(x, g, b, eps=1e-05):
            m = jnp.mean(x, axis=-1, keepdims=True)
            v = jnp.mean(jnp.square(x - m), axis=-1, keepdims=True)
            return (x - m) / jnp.sqrt(v + eps) * g + b

        def _heads(x):
            b, s, _ = x.shape
            return x.reshape(b, s, H, D).transpose(0, 2, 1, 3)

        def _mha(s, t, kv_w, q_w, o_w, o_b, mask):
            kv = s @ kv_w
            k, v = jnp.split(kv, 2, axis=-1)
            q = t @ q_w
            k, v, q = (_heads(k), _heads(v), _heads(q))
            scores = jnp.einsum('bhqd,bhkd->bhqk', q, k) * D ** (-0.5)
            scores = jnp.where(mask[:, None] == 0, jnp.float32(-1000000000.0), scores)
            attn = jax.nn.softmax(scores, axis=-1)
            o = jnp.einsum('bhqk,bhkd->bhqd', attn, v)
            o = o.transpose(0, 2, 1, 3).reshape(t.shape[0], t.shape[1], H * D)
            return o @ o_w + o_b
        key = jax.random.key(seed)
        ks = jax.random.split(key, 18)
        sc = 0.02
        inp = {'src': jax.random.normal(ks[0], (B, SS, SD), jnp.float32), 'tgt': jax.random.normal(ks[1], (B, ST, TD), jnp.float32), 'tgt_mask': jnp.broadcast_to(jnp.tril(jnp.ones((ST, ST), jnp.int32)), (B, ST, ST)), 'src_mask': jnp.ones((B, 1, SS), jnp.int32), 'norm_g': jnp.ones((TD,), jnp.float32), 'norm_b': jnp.zeros((TD,), jnp.float32), 'sa_kv': jax.random.normal(ks[2], (L, TD, 2 * H * D), jnp.float32) * sc, 'sa_q': jax.random.normal(ks[3], (L, TD, H * D), jnp.float32) * sc, 'sa_ow': jax.random.normal(ks[4], (L, H * D, TD), jnp.float32) * sc, 'sa_ob': jnp.zeros((L, TD), jnp.float32), 'ca_kv': jax.random.normal(ks[5], (L, SD, 2 * H * D), jnp.float32) * sc, 'ca_q': jax.random.normal(ks[6], (L, TD, H * D), jnp.float32) * sc, 'ca_ow': jax.random.normal(ks[7], (L, H * D, TD), jnp.float32) * sc, 'ca_ob': jnp.zeros((L, TD), jnp.float32), 'ff_w1': jax.random.normal(ks[8], (L, TD, FF), jnp.float32) * sc, 'ff_b1': jnp.zeros((L, FF), jnp.float32), 'ff_w2': jax.random.normal(ks[9], (L, FF, TD), jnp.float32) * sc, 'ff_b2': jnp.zeros((L, TD), jnp.float32), 'pre_g': jnp.ones((L, TD), jnp.float32), 'pre_b': jnp.zeros((L, TD), jnp.float32)}
        return inp
    _L2_xattn_all = _L2_xattn_setup()
    _L2_xattn_in = {k: v for k, v in _L2_xattn_all.items() if k in ('norm_g', 'norm_b', 'sa_kv', 'sa_q', 'sa_ow', 'sa_ob', 'ca_kv', 'ca_q', 'ca_ow', 'ca_ob', 'ff_w1', 'ff_b1', 'ff_w2', 'ff_b2', 'pre_g', 'pre_b')}
    del _L2_xattn_all

    def _L3_xattn_setup():
        import jax, jax.numpy as jnp
        import numpy as np
        B, T, E = (8, 512, 128)
        M, L = (32, 64)
        EPS = 1e-06
        key = jax.random.key(seed)
        ks = jax.random.split(key, 5)
        return {'emb': jax.random.normal(ks[0], (B, T, E), dtype=jnp.float32), 'latent': jax.random.normal(ks[1], (B, M, L), dtype=jnp.float32), 'Wq': jax.random.normal(ks[2], (E, E), dtype=jnp.float32) * (1.0 / np.sqrt(E)), 'bq': jnp.zeros((E,), dtype=jnp.float32), 'Wk': jax.random.normal(ks[3], (L, E), dtype=jnp.float32) * (1.0 / np.sqrt(L)), 'bk': jnp.zeros((E,), dtype=jnp.float32), 'Wv': jax.random.normal(ks[4], (L, E), dtype=jnp.float32) * (1.0 / np.sqrt(L)), 'bv': jnp.zeros((E,), dtype=jnp.float32), 'gamma': jnp.ones((E,), dtype=jnp.float32), 'beta': jnp.zeros((E,), dtype=jnp.float32)}
    _L3_xattn_all = _L3_xattn_setup()
    _L3_xattn_in = {k: v for k, v in _L3_xattn_all.items() if k in ('Wq', 'bq', 'Wk', 'bk', 'Wv', 'bv', 'gamma', 'beta')}
    del _L3_xattn_all
    return {'x': x, 'ctx_512': ctx_512, 'mask_BxSxS_ik0': mask_BxSxS_ik0, 'mask_Bx1xS2_if1': mask_Bx1xS2_if1, 'L0_xattn_Wq': _L0_xattn_in['Wq'], 'L0_xattn_bq': _L0_xattn_in['bq'], 'L0_xattn_Wk': _L0_xattn_in['Wk'], 'L0_xattn_bk': _L0_xattn_in['bk'], 'L0_xattn_Wv': _L0_xattn_in['Wv'], 'L0_xattn_bv': _L0_xattn_in['bv'], 'L0_xattn_gamma': _L0_xattn_in['gamma'], 'L0_xattn_beta': _L0_xattn_in['beta'], 'L1_xattn_Wq': _L1_xattn_in['Wq'], 'L1_xattn_bq': _L1_xattn_in['bq'], 'L1_xattn_Wk': _L1_xattn_in['Wk'], 'L1_xattn_bk': _L1_xattn_in['bk'], 'L1_xattn_Wv': _L1_xattn_in['Wv'], 'L1_xattn_bv': _L1_xattn_in['bv'], 'L1_xattn_Wo': _L1_xattn_in['Wo'], 'L1_xattn_bo': _L1_xattn_in['bo'], 'L2_xattn_norm_g': _L2_xattn_in['norm_g'], 'L2_xattn_norm_b': _L2_xattn_in['norm_b'], 'L2_xattn_sa_kv': _L2_xattn_in['sa_kv'], 'L2_xattn_sa_q': _L2_xattn_in['sa_q'], 'L2_xattn_sa_ow': _L2_xattn_in['sa_ow'], 'L2_xattn_sa_ob': _L2_xattn_in['sa_ob'], 'L2_xattn_ca_kv': _L2_xattn_in['ca_kv'], 'L2_xattn_ca_q': _L2_xattn_in['ca_q'], 'L2_xattn_ca_ow': _L2_xattn_in['ca_ow'], 'L2_xattn_ca_ob': _L2_xattn_in['ca_ob'], 'L2_xattn_ff_w1': _L2_xattn_in['ff_w1'], 'L2_xattn_ff_b1': _L2_xattn_in['ff_b1'], 'L2_xattn_ff_w2': _L2_xattn_in['ff_w2'], 'L2_xattn_ff_b2': _L2_xattn_in['ff_b2'], 'L2_xattn_pre_g': _L2_xattn_in['pre_g'], 'L2_xattn_pre_b': _L2_xattn_in['pre_b'], 'L3_xattn_Wq': _L3_xattn_in['Wq'], 'L3_xattn_bq': _L3_xattn_in['bq'], 'L3_xattn_Wk': _L3_xattn_in['Wk'], 'L3_xattn_bk': _L3_xattn_in['bk'], 'L3_xattn_Wv': _L3_xattn_in['Wv'], 'L3_xattn_bv': _L3_xattn_in['bv'], 'L3_xattn_gamma': _L3_xattn_in['gamma'], 'L3_xattn_beta': _L3_xattn_in['beta']}

def reference(x, ctx_512, mask_BxSxS_ik0, mask_Bx1xS2_if1, L0_xattn_Wq, L0_xattn_bq, L0_xattn_Wk, L0_xattn_bk, L0_xattn_Wv, L0_xattn_bv, L0_xattn_gamma, L0_xattn_beta, L1_xattn_Wq, L1_xattn_bq, L1_xattn_Wk, L1_xattn_bk, L1_xattn_Wv, L1_xattn_bv, L1_xattn_Wo, L1_xattn_bo, L2_xattn_norm_g, L2_xattn_norm_b, L2_xattn_sa_kv, L2_xattn_sa_q, L2_xattn_sa_ow, L2_xattn_sa_ob, L2_xattn_ca_kv, L2_xattn_ca_q, L2_xattn_ca_ow, L2_xattn_ca_ob, L2_xattn_ff_w1, L2_xattn_ff_b1, L2_xattn_ff_w2, L2_xattn_ff_b2, L2_xattn_pre_g, L2_xattn_pre_b, L3_xattn_Wq, L3_xattn_bq, L3_xattn_Wk, L3_xattn_bk, L3_xattn_Wv, L3_xattn_bv, L3_xattn_gamma, L3_xattn_beta):
    import jax
    import jax.numpy as jnp

    def _L0_xattn_ref(emb, latent, Wq, bq, Wk, bk, Wv, bv, gamma, beta):
        import jax, jax.numpy as jnp
        import numpy as np
        B, T, E = (8, 512, 128)
        M, L = (32, 64)
        EPS = 1e-06
        q = jnp.einsum('bte,ef->btf', emb, Wq) + bq
        k = jnp.einsum('bml,le->bme', latent, Wk) + bk
        v = jnp.einsum('bml,le->bme', latent, Wv) + bv
        scale = 1.0 / jnp.sqrt(jnp.asarray(E, dtype=q.dtype))
        w = jnp.einsum('bte,bme->btm', q, k) * scale
        w = jax.nn.softmax(w, axis=1)
        pred = jnp.einsum('btm,bme->bte', w, v)
        x = pred + emb
        mu = jnp.mean(x, axis=-1, keepdims=True)
        var = jnp.var(x, axis=-1, keepdims=True)
        return (x - mu) * jax.lax.rsqrt(var + EPS) * gamma + beta

    def _L1_xattn_ref(query, key, Wq, bq, Wk, bk, Wv, bv, Wo, bo):
        import jax, jax.numpy as jnp
        import numpy as np
        QUERY_DIM = 128
        KEY_DIM = 64
        HIDDEN_DIM = 128
        B, LQ, LK = (8, 256, 256)
        scale = HIDDEN_DIM ** (-0.5)
        Q = jnp.einsum('bqd,dh->bqh', query, Wq) + bq
        K = jnp.einsum('bkd,dh->bkh', key, Wk) + bk
        V = jnp.einsum('bkd,dh->bkh', key, Wv) + bv
        scores = jnp.einsum('bqh,bkh->bqk', Q, K) * scale
        weights = jax.nn.softmax(scores, axis=-1)
        attended = jnp.einsum('bqk,bkh->bqh', weights, V)
        out = jnp.einsum('bqh,hd->bqd', attended, Wo) + bo
        return query + out

    def _L2_xattn_ref(src, tgt, tgt_mask, src_mask, norm_g, norm_b, sa_kv, sa_q, sa_ow, sa_ob, ca_kv, ca_q, ca_ow, ca_ob, ff_w1, ff_b1, ff_w2, ff_b2, pre_g, pre_b):
        import jax, jax.numpy as jnp
        import numpy as np
        B, ST, SS = (8, 64, 72)
        TD, SD = (128, 64)
        L, H, D, FF = (6, 16, 64, 512)

        def _ln(x, g, b, eps=1e-05):
            m = jnp.mean(x, axis=-1, keepdims=True)
            v = jnp.mean(jnp.square(x - m), axis=-1, keepdims=True)
            return (x - m) / jnp.sqrt(v + eps) * g + b

        def _heads(x):
            b, s, _ = x.shape
            return x.reshape(b, s, H, D).transpose(0, 2, 1, 3)

        def _mha(s, t, kv_w, q_w, o_w, o_b, mask):
            kv = s @ kv_w
            k, v = jnp.split(kv, 2, axis=-1)
            q = t @ q_w
            k, v, q = (_heads(k), _heads(v), _heads(q))
            scores = jnp.einsum('bhqd,bhkd->bhqk', q, k) * D ** (-0.5)
            scores = jnp.where(mask[:, None] == 0, jnp.float32(-1000000000.0), scores)
            attn = jax.nn.softmax(scores, axis=-1)
            o = jnp.einsum('bhqk,bhkd->bhqd', attn, v)
            o = o.transpose(0, 2, 1, 3).reshape(t.shape[0], t.shape[1], H * D)
            return o @ o_w + o_b
        stacked = (sa_kv, sa_q, sa_ow, sa_ob, ca_kv, ca_q, ca_ow, ca_ob, ff_w1, ff_b1, ff_w2, ff_b2, pre_g, pre_b)

        def step(t, p):
            skv, sq, sow, sob, ckv, cq, cow, cob, w1, b1, w2, b2, pg, pb = p
            tn = _ln(t, norm_g, norm_b)
            t = _mha(tn, tn, skv, sq, sow, sob, tgt_mask) + t
            tn = _ln(t, norm_g, norm_b)
            t = _mha(src, tn, ckv, cq, cow, cob, src_mask) + t
            tn = _ln(t, pg, pb)
            t = t + (jax.nn.relu(tn @ w1 + b1) @ w2 + b2)
            return (t, None)
        out, _ = jax.lax.scan(step, tgt, stacked)
        return out

    def _L3_xattn_ref(emb, latent, Wq, bq, Wk, bk, Wv, bv, gamma, beta):
        import jax, jax.numpy as jnp
        import numpy as np
        B, T, E = (8, 512, 128)
        M, L = (32, 64)
        EPS = 1e-06
        q = jnp.einsum('bte,ef->btf', emb, Wq) + bq
        k = jnp.einsum('bml,le->bme', latent, Wk) + bk
        v = jnp.einsum('bml,le->bme', latent, Wv) + bv
        scale = 1.0 / jnp.sqrt(jnp.asarray(E, dtype=q.dtype))
        w = jnp.einsum('bte,bme->btm', q, k) * scale
        w = jax.nn.softmax(w, axis=1)
        pred = jnp.einsum('btm,bme->bte', w, v)
        x = pred + emb
        mu = jnp.mean(x, axis=-1, keepdims=True)
        var = jnp.var(x, axis=-1, keepdims=True)
        return (x - mu) * jax.lax.rsqrt(var + EPS) * gamma + beta
    x = _L0_xattn_ref(x, ctx_512, L0_xattn_Wq, L0_xattn_bq, L0_xattn_Wk, L0_xattn_bk, L0_xattn_Wv, L0_xattn_bv, L0_xattn_gamma, L0_xattn_beta)
    x = _L1_xattn_ref(x, ctx_512, L1_xattn_Wq, L1_xattn_bq, L1_xattn_Wk, L1_xattn_bk, L1_xattn_Wv, L1_xattn_bv, L1_xattn_Wo, L1_xattn_bo)
    x = _L2_xattn_ref(ctx_512, x, mask_BxSxS_ik0, mask_Bx1xS2_if1, L2_xattn_norm_g, L2_xattn_norm_b, L2_xattn_sa_kv, L2_xattn_sa_q, L2_xattn_sa_ow, L2_xattn_sa_ob, L2_xattn_ca_kv, L2_xattn_ca_q, L2_xattn_ca_ow, L2_xattn_ca_ob, L2_xattn_ff_w1, L2_xattn_ff_b1, L2_xattn_ff_w2, L2_xattn_ff_b2, L2_xattn_pre_g, L2_xattn_pre_b)
    x = _L3_xattn_ref(x, ctx_512, L3_xattn_Wq, L3_xattn_bq, L3_xattn_Wk, L3_xattn_bk, L3_xattn_Wv, L3_xattn_bv, L3_xattn_gamma, L3_xattn_beta)
    return x

_drawn_inputs = setup_inputs


def setup_inputs(seed=0):
    import zlib

    import numpy as np

    out = dict(_drawn_inputs(seed))
    spreads = {'L0_xattn_bq': (0.0, 2.0),
     'L0_xattn_bk': (0.0, 0.8),
     'L0_xattn_bv': (0.0, 0.485),
     'L0_xattn_gamma': (1.0, 0.2),
     'L0_xattn_beta': (0.0, 0.1),
     'L2_xattn_norm_g': (1.0, 0.6),
     'L2_xattn_norm_b': (0.0, 0.1),
     'L2_xattn_sa_ob': (0.0, 0.1),
     'L2_xattn_ca_ob': (0.0, 0.1),
     'L2_xattn_ff_b1': (0.0, 0.1),
     'L2_xattn_ff_b2': (0.0, 0.1),
     'L2_xattn_pre_g': (1.0, 0.536),
     'L2_xattn_pre_b': (0.0, 0.573),
     'L3_xattn_bq': (0.0, 2.0),
     'L3_xattn_bk': (0.0, 0.8),
     'L3_xattn_bv': (0.0, 0.602),
     'L3_xattn_gamma': (1.0, 0.2),
     'L3_xattn_beta': (0.0, 0.1)}
    factors = {'L1_xattn_Wq': 2.692,
     'L1_xattn_bq': 8.0,
     'L1_xattn_Wk': 2.887,
     'L1_xattn_bk': 64.0,
     'L2_xattn_sa_q': 8.0,
     'L2_xattn_ca_q': 25.517}
    for name, (base, spread) in spreads.items():
        noise = np.random.default_rng([zlib.crc32(name.encode()), seed]).standard_normal(out[name].shape)
        drawn = base * np.exp(spread * noise) if base else spread * noise
        out[name] = jnp.asarray(drawn.astype(out[name].dtype))
    for name, factor in factors.items():
        out[name] = (out[name] * factor).astype(out[name].dtype)
    return out
```

```python
from contextlib import ExitStack

import concourse.bass as bass
from concourse import mybir

F32 = mybir.dt.float32
I32 = mybir.dt.int32
ALU = mybir.AluOpType
ACT = mybir.ActivationFunctionType
AX = mybir.AxisListType.X

B, T, E = 2, 512, 128
M, CD = 77, 64
L, H, D, FF = 6, 16, 64, 512
P = 128
NT = B * T // P
TB = T // P
NPAIR = H * D // P
NF = FF // P
KEYS = T - P
BIG = 1.0e30
PAD = 3.0e38
EPS_LATENT, EPS_DEC = 1e-6, 1e-5
RSQRT_SEED = 0x5F3759DF
NEWTON = 4


class Phase:

    def __init__(self, name, key_tiles, key_base):
        self.name, self.key_tiles, self.key_base = name, key_tiles, key_base
        self.wide = key_tiles > 1
        self.per_unit = TB if self.wide else 1
        self.per_pair = 4 * self.per_unit
        self.chunks = NPAIR * self.per_pair
        if self.wide:
            self.pieces = ["q0", "k0", "v0", "q1", "k1", "v1"]
            at = [2, 4, 6, 8, 10, 12]
        else:
            self.pieces = ["q0", "k", "v", "q1"]
            at = [0, 0, 1, 1]
        self.plan = [[] for _ in range(self.chunks + 2)]
        for p in range(NPAIR):
            for b in range(B):
                end = p * self.per_pair + (b + 1) * 2 * self.per_unit - 1
                self.plan[end + 2].append((p, f"y{b}"))
        for p in range(1, NPAIR):
            for piece, n in zip(self.pieces, at):
                self.plan[(p - 1) * self.per_pair + n].append((p, piece))
        self.first = [(0, piece) for piece in self.pieces]
        order = self.first + [e for step in self.plan for e in step]
        self.index = {e: i for i, e in enumerate(order)}
        self.per_bank = len(order) // 2
        assert len(order) == 2 * self.per_bank

    def bank(self, event):
        return self.index[event] % 2

    def count(self, event):
        return self.index[event] // 2 + 1

    def where(self, n):
        p, r = divmod(n, self.per_pair)
        u, qt = divmod(r, self.per_unit)
        return p, u, u // 2, u % 2, qt

    def ends_unit(self, n):
        return 0 <= n < self.chunks and (n + 1) % self.per_unit == 0

    def piece_of(self, kind, b):
        return f"{kind}{b}" if self.wide or kind == "q" else kind


SELF_ALL = Phase("sa4", TB, 0)
SELF_LAST = Phase("sa1", 1, KEYS)
CROSS = Phase("ca", 1, 0)


def build(nc, a, out, force_all=False):
    with ExitStack() as ctx:
        def sb(name, shape, dt=F32):
            return ctx.enter_context(nc.sbuf_tensor(name, shape, dt))

        sems = {}

        def sem(name):
            if name not in sems:
                sems[name] = ctx.enter_context(nc.semaphore(name))
            return sems[name]

        ident = sb("ident", [P, P])
        ones = sb("ones", [P, 1])
        X = sb("X", [P, NT, E])
        XN = sb("XN", [P, NT, E])
        XT = sb("XT", [P, B * T])
        ctx_in = sb("ctx_in", [P, B, CD])
        ctxT = sb("ctxT", [CD, B, P])
        mask_i = sb("mask_i", [P, NT, T], I32)
        self_bias = sb("self_bias", [P, NT, T])
        cmask_i = sb("cmask_i", [P, B, M], I32)
        cross_bias = sb("cross_bias", [P, B, P])
        stats = sb("stats", [P, NT, 6])
        mv = sb("mv", [P, NT, 2])
        veps = sb("veps", [P, NT])
        rstd = sb("rstd", [P, NT])
        newton = sb("newton", [P, NT])
        qT = sb("qT", [P, 2, B * T])
        kz = sb("kz", [P, 2, 2, B * T])
        vv = sb("vv", [P, 2, NT, P])
        Sm = sb("Sm", [P, 2, T])
        Pb = sb("Pb", [P, 2, T])
        PT = sb("PT", [P, 2, TB, T])
        mn = sb("mn", [P, 2, TB])
        sums = sb("sums", [P, 2, TB])
        rsum = sb("rsum", [P, 2, TB])
        oT = sb("oT", [P, 2, T])
        hT = sb("hT", [P, B, NF, T])
        saq, sakv = sb("saq", [P, H * D]), sb("sakv", [P, 2 * H * D])
        saow = sb("saow", [P, NPAIR, E])
        caq, cakv = sb("caq", [P, H * D]), sb("cakv", [CD, 2 * H * D])
        caow = sb("caow", [P, NPAIR, E])
        w1, w2 = sb("w1", [P, FF]), sb("w2", [P, NF, E])
        sob, cob, b2 = sb("sob", [P, E]), sb("cob", [P, E]), sb("b2", [P, E])
        b1 = sb("b1", [P, NF])
        pre_g, pre_b = sb("pre_g", [P, 1]), sb("pre_b", [P, 1])
        norm_g, norm_b = sb("norm_g", [P, 1]), sb("norm_b", [P, 1])
        OUTER = ["L0", "L1", "L3"]
        wq = {s: sb(f"{s}wq", [P, P]) for s in OUTER}
        wk = {s: sb(f"{s}wk", [CD, P]) for s in OUTER}
        wv = {s: sb(f"{s}wv", [CD, P]) for s in OUTER}
        bq = {s: sb(f"{s}bq", [P, 1]) for s in OUTER}
        bk = {s: sb(f"{s}bk", [P, 1]) for s in OUTER}
        bv = {s: sb(f"{s}bv", [P, P]) for s in OUTER}
        gam = {s: sb(f"{s}gam", [P, P]) for s in ("L0", "L3")}
        bet = {s: sb(f"{s}bet", [P, P]) for s in ("L0", "L3")}
        wo1, bo1 = sb("wo1", [P, P]), sb("bo1", [P, P])
        kT = sb("kT", [P, B, P])
        vo = sb("vo", [P, B, P])
        omax = sb("omax", [P, NT])
        onmx = sb("onmx", [P, NT])
        osum = sb("osum", [P, NT])
        orec = sb("orec", [P, NT])
        OP = sb("OP", [P, B, T])
        carrier = sb("carrier", [P, 1])
        bad = sb("bad", [P, NT, 2])
        badp = sb("badp", [P, 1])
        flag_f = sb("flag_f", [1, 1])
        flag = sb("flag", [1, 1], I32)

        def bank(name):
            return ctx.enter_context(nc.psum_tensor(name, [P, T], F32))

        S_ps = [bank("S0"), bank("S1")]
        T_ps = [bank("T0"), bank("T1")]
        O_ps = [bank("O0"), bank("O1")]
        W_ps = [bank("W0"), bank("W1")]

        def tiles(ap):
            return ap.rearrange("p (t e) -> p t e", e=P)

        def row(v):
            return v.rearrange("(a n) -> a n", a=1).broadcast_to([P, v.shape[0]])

        def col(v):
            return v.rearrange("(p a) -> p a", a=1)

        block = ctx.enter_context(nc.Block())

        @block.sync
        def _(sp):
            sp.dma_start(X[:], a["x"].rearrange("b (t p) e -> p (b t) e", p=P)).then_inc(sem("x_in"), 16)
            for b in range(B):
                sp.dma_start(ctx_in[0:M, b, :], a["ctx_512"][b]).then_inc(sem("ctx_in"), 16)
            for s in OUTER:
                w = f"{s}_xattn_"
                for dst, src in ((wq[s][:], a[w + "Wq"]), (wk[s][:], a[w + "Wk"]), (wv[s][:], a[w + "Wv"]),
                                 (bq[s][:], col(a[w + "bq"])), (bk[s][:], col(a[w + "bk"])),
                                 (bv[s][:], row(a[w + "bv"]))):
                    sp.dma_start(dst, src).then_inc(sem("outer_in" + s), 16)
                if s == "L1":
                    sp.dma_start(wo1[:], a[w + "Wo"]).then_inc(sem("outer_inL1"), 16)
                    sp.dma_start(bo1[:], row(a[w + "bo"])).then_inc(sem("outer_inL1"), 16)
                else:
                    sp.dma_start(gam[s][:], row(a[w + "gamma"])).then_inc(sem("outer_in" + s), 16)
                    sp.dma_start(bet[s][:], row(a[w + "beta"])).then_inc(sem("outer_in" + s), 16)
                if s == "L0":
                    sp.dma_start(mask_i[:], a["mask_BxSxS_ik0"].rearrange("b (t p) k -> p (b t) k", p=P))\
                      .then_inc(sem("mask_in"), 16)
                    sp.dma_start(cmask_i[:], a["mask_Bx1xS2_if1"].rearrange("b a m -> a b m").broadcast_to([P, B, M]))\
                      .then_inc(sem("mask_in"), 16)
                    sp.dma_start(norm_g[:], col(a["L2_xattn_norm_g"])).then_inc(sem("norm_in"), 16)
                    sp.dma_start(norm_b[:], col(a["L2_xattn_norm_b"])).then_inc(sem("norm_in"), 16)

            def layer(name, l):
                v = a["L2_xattn_" + name]
                v = v[bass.ds(l, 1)]
                return v.rearrange("a p n -> p (a n)") if len(v.shape) == 3 else v

            def load_self(l):
                for dst, src in ((saq[:], layer("sa_q", l)), (sakv[:], layer("sa_kv", l)),
                                 (saow[:], a["L2_xattn_sa_ow"][bass.ds(l, 1)].rearrange("a (g p) n -> p (a g) n", p=P)),
                                 (sob[:], layer("sa_ob", l).broadcast_to([P, E]))):
                    sp.dma_start(dst, src).then_inc(sem("self_w"), 16)

            def load_cross(l):
                for dst, src in ((caq[:], layer("ca_q", l)), (cakv[:], layer("ca_kv", l)),
                                 (caow[:], a["L2_xattn_ca_ow"][bass.ds(l, 1)].rearrange("a (g p) n -> p (a g) n", p=P)),
                                 (cob[:], layer("ca_ob", l).broadcast_to([P, E]))):
                    sp.dma_start(dst, src).then_inc(sem("cross_w"), 16)

            def load_ff(l):
                for dst, src in ((w1[:], layer("ff_w1", l)),
                                 (w2[:], a["L2_xattn_ff_w2"][bass.ds(l, 1)].rearrange("a (g p) n -> p (a g) n", p=P)),
                                 (b2[:], layer("ff_b2", l).broadcast_to([P, E])),
                                 (b1[:], layer("ff_b1", l).rearrange("a (g p) -> p (a g)", p=P)),
                                 (pre_g[:], layer("pre_g", l).rearrange("a p -> p a")),
                                 (pre_b[:], layer("pre_b", l).rearrange("a p -> p a"))):
                    sp.dma_start(dst, src, allow_slow_non_contiguous=True).then_inc(sem("ff_w"), 16)

            load_self(0)
            load_cross(0)
            load_ff(0)
            with sp.Fori(0, L - 1) as l:
                sp.wait_ge(sem("self_done"), l + 1)
                load_self(l + 1)
                sp.wait_ge(sem("cross_done"), l + 1)
                load_cross(l + 1)
                sp.wait_ge(sem("ff_done"), l + 1)
                load_ff(l + 1)
            for b in range(B):
                sp.wait_ge(sem("out_ready"), b + 1)
                sp.dma_start(out[b].rearrange("(t p) e -> p t e", p=P), X[:, b * TB:(b + 1) * TB, :])\
                  .then_inc(sem("out_done"), 16)
            sp.wait_ge(sem("out_done"), 32)

        @block.gpsimd
        def _(gp):
            nc.gpsimd.memset(ident[:], 0.0).then_inc(sem("gp_zero"), 1)
            nc.gpsimd.memset(ones[:], 1.0).then_inc(sem("gp_zero"), 1)
            nc.gpsimd.memset(ctxT[:], 0.0).then_inc(sem("gp_zero"), 1)
            nc.gpsimd.memset(cross_bias[:], PAD).then_inc(sem("gp_zero"), 1)
            gp.wait_ge(sem("gp_zero"), 4)
            nc.gpsimd.affine_select(out=ident[:], in_=ident[:], compare_op=ALU.not_equal, fill=1.0, base=0,
                                    pattern=[[-1, P]], channel_multiplier=1).then_inc(sem("consts"), 1)

        @block.tensor
        def _(pe):
            def transposes(src, bank, n, name):
                for t in range(TB):
                    last = nc.tensor.transpose(bank[:, t * P:(t + 1) * P], src[:, n * TB + t, :], ident[:])
                last.then_inc(sem(name), 1)

            def to_features(src, name):
                for b in range(B):
                    pe.wait_ge(sem(name + "_src"), b + 1)
                    transposes(src, T_ps[b], b, name + "_turned")

            def outer_projections(s, full, nb):
                pe.wait_ge(sem("outer_in" + s), 16 * 8)
                for b in range(B):
                    pe.wait_ge(sem(nb + "_xt"), b + 1)
                    nc.tensor.matmul(W_ps[b][:], wq[s][:], XT[:, b * T:(b + 1) * T], start=True, stop=True)\
                      .then_inc(sem(s + "_q"), 1)
                nc.tensor.matmul(S_ps[0][:, 0:B * P], wk[s][:], ctxT[:].rearrange("c b m -> c (b m)"),
                                 start=True, stop=True).then_inc(sem(s + "_k"), 1)
                for b in range(B):
                    last = nc.tensor.matmul(S_ps[1][:, b * P:(b + 1) * P], ctxT[:, b, :], wv[s][:],
                                            start=True, stop=True)
                last.then_inc(sem(s + "_v"), 1)

            def token_softmax(s, nb):
                outer_projections(s, None, nb)
                for b in range(B):
                    pe.wait_ge(sem(s + "_qk_sb"), 3 + 0 * b)
                    nc.tensor.matmul(O_ps[b][0:M, :], kT[:, b, 0:M], qT[:, 0, b * T:(b + 1) * T],
                                     start=True, stop=True).then_inc(sem(s + "_scores"), 1)
                for b in range(B):
                    pe.wait_ge(sem(s + "_weights"), b + 1)
                    pe.wait_ge(sem(s + "_v_sb"), 1)
                    for t in range(TB):
                        last = nc.tensor.matmul(W_ps[b][:, t * P:(t + 1) * P], OP[0:M, b, t * P:(t + 1) * P],
                                                vo[0:M, b, :], start=True, stop=True)
                    last.then_inc(sem(s + "_pred"), 1)

            pe.wait_ge(sem("consts"), 1)
            pe.wait_ge(sem("ctx_in"), 16 * B)
            for b in range(B):
                last = nc.tensor.transpose(S_ps[0][0:CD, b * P:b * P + M], ctx_in[0:M, b, :], ident[0:M, 0:M])
            last.then_inc(sem("ctx_turned"), 1)
            pe.wait_ge(sem("x_in"), 16)
            for b in range(B):
                transposes(X, T_ps[b], b, "A_turned")
            pe.wait_ge(sem("ctx_sb"), 1)
            token_softmax("L0", "A")
            to_features(X, "B")
            outer_projections("L1", None, "B")
            pe.wait_ge(sem("L1_qk_sb"), 3)
            for b in range(B):
                for t in range(TB):
                    last = nc.tensor.matmul(O_ps[b][:, t * P:t * P + M],
                                            qT[:, 0, (b * TB + t) * P:(b * TB + t + 1) * P], kT[:, b, 0:M],
                                            start=True, stop=True)
                last.then_inc(sem("L1_scores"), 1)
            for b in range(B):
                pe.wait_ge(sem("L1_weights"), b + 1)
                for t in range(TB):
                    last = nc.tensor.transpose(T_ps[b][0:M, t * P:(t + 1) * P], XN[:, b * TB + t, 0:M], ident[:])
                last.then_inc(sem("L1_turned"), 1)
            pe.wait_ge(sem("L1_v_sb"), 1)
            for b in range(B):
                pe.wait_ge(sem("L1_wT"), b + 1)
                nc.tensor.matmul(S_ps[b][:], vo[0:M, b, :], OP[0:M, b, :], start=True, stop=True)\
                  .then_inc(sem("L1_att"), 1)
            for b in range(B):
                pe.wait_ge(sem("L1_att_sb"), b + 1)
                for t in range(TB):
                    last = nc.tensor.matmul(W_ps[b][:, t * P:(t + 1) * P], oT[:, b, t * P:(t + 1) * P], wo1[:],
                                            start=True, stop=True)
                last.then_inc(sem("L1_out"), 1)
            pe.wait_ge(sem("bad_rows"), 1)
            pe.wait_ge(sem("L1_done"), 1)
            nc.tensor.matmul(O_ps[0][0:1, 0:1], badp[:], ones[:], start=True, stop=True).then_inc(sem("bad_sum"), 1)

            def attention(ph, l):
                cross = ph is CROSS
                wq_, wkv, wo_ = (caq, cakv, caow) if cross else (saq, sakv, saow)
                N, half = ph.chunks, ph.per_bank

                def work(event):
                    p, what = event
                    bk_ = ph.bank(event)
                    if ph.count(event) > 1:
                        pe.wait_ge(sem(f"{ph.name}_work_free{bk_}"), l * half + ph.count(event) - 1)
                    w, slot = W_ps[bk_], p % 2
                    heads = slice(p * P, (p + 1) * P)
                    vcols = slice(H * D + p * P, H * D + (p + 1) * P)
                    b = int(what[1]) if what[1:] else 0
                    if what[0] == "q":
                        last = nc.tensor.matmul(w[:], wq_[:, heads], XT[:, b * T:(b + 1) * T], start=True, stop=True)
                    elif what[0] == "k":
                        if ph.wide:
                            src, n = XT[:, b * T:(b + 1) * T], T
                        elif cross:
                            src, n = ctxT[:].rearrange("c b m -> c (b m)"), B * P
                        else:
                            src, n = XT[:].rearrange("c (b t) -> c b t", b=B)[:, :, KEYS:T], B * P
                        dst = w[:, 0:n] if ph.wide or cross else w[:, 0:n].rearrange("p (b t) -> p b t", b=B)
                        last = nc.tensor.matmul(dst, wkv[:, heads], src, start=True, stop=True)
                    elif what[0] == "v":
                        if ph.wide:
                            srcs = [XT[:, (b * TB + t) * P:(b * TB + t + 1) * P] for t in range(TB)]
                        elif cross:
                            srcs = [ctxT[:, i, :] for i in range(B)]
                        else:
                            srcs = [XT[:, i * T + KEYS:(i + 1) * T] for i in range(B)]
                        for t, src in enumerate(srcs):
                            last = nc.tensor.matmul(w[:, t * P:(t + 1) * P], src, wkv[:, vcols], start=True, stop=True)
                    else:
                        pe.wait_ge(sem(f"{ph.name}_att_sb"), l * B * NPAIR + p * B + b + 1)
                        for t in range(TB):
                            last = nc.tensor.matmul(w[:, t * P:(t + 1) * P], oT[:, b, t * P:(t + 1) * P],
                                                    wo_[:, p, :], start=True, stop=True)
                    last.then_inc(sem(f"{ph.name}_work_full{bk_}"), 1)

                def evacuated(event):
                    pe.wait_ge(sem(f"{ph.name}_work_free{ph.bank(event)}"), l * half + ph.count(event))

                def scores(n):
                    p, u, b, hh, qt = ph.where(n)
                    slot = p % 2
                    if hh == 0 and qt == 0:
                        evacuated((p, f"q{b}"))
                        evacuated((p, ph.piece_of("k", b)))
                    if n >= 2:
                        pe.wait_ge(sem(f"{ph.name}_masked"), l * N + n - 1)
                    if ph.wide:
                        q = b * TB + qt
                        last = nc.tensor.matmul(S_ps[n % 2][:], qT[:, slot, q * P:(q + 1) * P],
                                                kz[:, slot, hh, b * T:(b + 1) * T], start=True, stop=True)
                    else:
                        for t in range(TB):
                            q = b * TB + t
                            last = nc.tensor.matmul(S_ps[n % 2][:, t * P:(t + 1) * P], qT[:, slot, q * P:(q + 1) * P],
                                                    kz[:, slot, hh, b * P:(b + 1) * P], start=True, stop=True)
                    last.then_inc(sem(f"{ph.name}_scores"), 1)

                def turn(n):
                    pe.wait_ge(sem(f"{ph.name}_weights"), l * N + n + 1)
                    if n >= 2:
                        pe.wait_ge(sem(f"{ph.name}_turned_sb"), l * N + n - 1)
                    for t in range(TB):
                        last = nc.tensor.transpose(T_ps[n % 2][:, t * P:(t + 1) * P],
                                                   Pb[:, n % 2, t * P:(t + 1) * P], ident[:])
                    last.then_inc(sem(f"{ph.name}_turned"), 1)

                def attend(n):
                    p, u, b, hh, _ = ph.where(n)
                    unit = p * 4 + u
                    pe.wait_ge(sem(f"{ph.name}_turned_sb"), l * N + n + 1)
                    if hh == 0:
                        evacuated((p, ph.piece_of("v", b)))
                        if p:
                            pe.wait_ge(sem(f"{ph.name}_att_sb"), l * B * NPAIR + (p - 1) * B + b + 1)
                    for kt in range(ph.key_tiles):
                        tile = b * TB + kt if ph.wide else b
                        last = nc.tensor.matmul(O_ps[b][hh * D:(hh + 1) * D, :], vv[:, p % 2, tile, hh * D:(hh + 1) * D],
                                                PT[:, unit % 2, kt, :], start=(kt == 0), stop=(kt == ph.key_tiles - 1))
                    last.then_inc(sem(f"{ph.name}_attended"), 1)

                for event in ph.first:
                    work(event)
                scores(0)
                scores(1)
                for n in range(N + 2):
                    if n + 2 < N:
                        scores(n + 2)
                    if n < N:
                        turn(n)
                    if ph.ends_unit(n - 1):
                        attend(n - 1)
                    for event in ph.plan[n]:
                        work(event)

            def normed(k):
                for b in range(B):
                    pe.wait_ge(sem("xn_ready"), k * B + b + 1)
                    transposes(XN, T_ps[b], b, "xn_turned")

            pe.wait_ge(sem("kz_zero"), 2)
            pe.wait_ge(sem("flag"), 1)
            general = pe.value_load(flag[0:1, 0:1], min_val=0, max_val=1)
            with pe.Fori(0, L) as l:
                normed(l * 3)
                pe.wait_ge(sem("xt_ready"), (l * 3) * B + B)
                pe.wait_ge(sem("self_w"), 64 * l + 64)
                with pe.If(general > 0):
                    attention(SELF_ALL, l)
                with pe.Else():
                    attention(SELF_LAST, l)
                normed(l * 3 + 1)
                pe.wait_ge(sem("xt_ready"), (l * 3 + 1) * B + B)
                pe.wait_ge(sem("cross_w"), 64 * l + 64)
                attention(CROSS, l)
                normed(l * 3 + 2)
                pe.wait_ge(sem("ff_w"), 96 * l + 96)
                for i in range(B * NF):
                    b, f = divmod(i, NF)
                    if f == 0:
                        pe.wait_ge(sem("xt_ready"), (l * 3 + 2) * B + b + 1)
                    if i >= 2:
                        pe.wait_ge(sem("hidden_sb"), l * B * NF + i - 1)
                    nc.tensor.matmul(S_ps[i % 2][:], w1[:, f * P:(f + 1) * P], XT[:, b * T:(b + 1) * T],
                                     start=True, stop=True).then_inc(sem("hidden"), 1)
                for b in range(B):
                    pe.wait_ge(sem("hidden_sb"), l * B * NF + (b + 1) * NF)
                    for t in range(TB):
                        for f in range(NF):
                            last = nc.tensor.matmul(O_ps[b][:, t * P:(t + 1) * P], hT[:, b, f, t * P:(t + 1) * P],
                                                    w2[:, f, :], start=(f == 0), stop=(f == NF - 1))
                    last.then_inc(sem("ff_out"), 1)
            to_features(X, "C")
            token_softmax("L3", "C")

        @block.scalar
        def _(act):
            def features(name, bias=None):
                for b in range(B):
                    act.wait_ge(sem(name + "_turned"), b + 1)
                    nc.scalar.activation(XT[:, b * T:(b + 1) * T], T_ps[b][:], ACT.Copy).then_inc(sem(name + "_xt"), 1)

            def outer_evacuations(s):
                act.wait_ge(sem("outer_in" + s), 16 * 8)
                for b in range(B):
                    act.wait_ge(sem(s + "_q"), b + 1)
                    nc.scalar.activation(qT[:, 0, b * T:(b + 1) * T], W_ps[b][:], ACT.Identity, bias=bq[s][:])\
                      .then_inc(sem(s + "_qk_sb"), 1)
                act.wait_ge(sem(s + "_k"), 1)
                nc.scalar.activation(kT[:].rearrange("p b m -> p (b m)"), S_ps[0][:, 0:B * P], ACT.Identity,
                                     bias=bk[s][:]).then_inc(sem(s + "_qk_sb"), 1)

            act.wait_ge(sem("ctx_turned"), 1)
            act.wait_ge(sem("consts"), 1)
            nc.scalar.activation(ctxT[:, :, 0:M], S_ps[0][0:CD, 0:B * P].rearrange("c (b m) -> c b m", b=B)[:, :, 0:M],
                                 ACT.Copy).then_inc(sem("ctx_sb"), 1)

            def token_softmax(s):
                outer_evacuations(s)
                for b in range(B):
                    act.wait_ge(sem(s + "_max"), b + 1)
                    nc.scalar.activation(OP[0:M, b, :], O_ps[b][0:M, :], ACT.Exp, bias=onmx[0:M, b:b + 1],
                                         scale=float(E) ** -0.5, accum_out=osum[0:M, b:b + 1])\
                      .then_inc(sem(s + "_exp"), 1)

            features("A")
            token_softmax("L0")
            features("B")
            outer_evacuations("L1")
            for b in range(B):
                act.wait_ge(sem("L1_max"), b + 1)
                for t in range(TB):
                    i = b * TB + t
                    last = nc.scalar.activation(XN[:, i, 0:M], O_ps[b][:, t * P:t * P + M], ACT.Exp,
                                                bias=onmx[:, i:i + 1], scale=float(E) ** -0.5,
                                                accum_out=osum[:, i:i + 1])
                last.then_inc(sem("L1_exp"), 1)
            for b in range(B):
                act.wait_ge(sem("L1_turned"), b + 1)
                nc.scalar.activation(OP[0:M, b, :], T_ps[b][0:M, :], ACT.Copy).then_inc(sem("L1_wT"), 1)
            for b in range(B):
                act.wait_ge(sem("L1_att"), b + 1)
                nc.scalar.activation(oT[:, b, :], S_ps[b][:], ACT.Copy).then_inc(sem("L1_att_sb"), 1)

            def attention(ph, l):
                N, half = ph.chunks, ph.per_bank

                def work(event):
                    p, what = event
                    if what != "q0":
                        return
                    bk_ = ph.bank(event)
                    act.wait_ge(sem(f"{ph.name}_work_full{bk_}"), l * half + ph.count(event))
                    nc.scalar.activation(qT[:, p % 2, 0:T], W_ps[bk_][:], ACT.Copy, scale=-float(D) ** -0.5)\
                      .then_inc(sem(f"{ph.name}_work_free{bk_}"), 1)

                def exponentials(n):
                    act.wait_ge(sem(f"{ph.name}_masked"), l * N + n + 1)
                    if n >= 2:
                        act.wait_ge(sem(f"{ph.name}_turned"), l * N + n - 1)
                    s = n % 2
                    w = T if ph.wide else P
                    for t in range(T // w):
                        last = nc.scalar.activation(Pb[:, s, t * w:(t + 1) * w], Sm[:, s, t * w:(t + 1) * w], ACT.Exp,
                                                    bias=mn[:, s, t:t + 1], scale=-1.0, accum_out=sums[:, s, t:t + 1])
                    last.then_inc(sem(f"{ph.name}_exp"), 1)

                def evacuate_turned(n):
                    p, u, b, hh, qt = ph.where(n)
                    unit = p * 4 + u
                    act.wait_ge(sem(f"{ph.name}_turned"), l * N + n + 1)
                    if unit >= 2 and qt == 0:
                        act.wait_ge(sem(f"{ph.name}_attended"), l * 4 * NPAIR + unit - 1)
                    if ph.wide:
                        dst, src = PT[:, unit % 2, :, qt * P:(qt + 1) * P], tiles(T_ps[n % 2][:])
                    else:
                        dst, src = PT[:, unit % 2, 0, :], T_ps[n % 2][:]
                    nc.scalar.activation(dst, src, ACT.Copy).then_inc(sem(f"{ph.name}_turned_sb"), 1)

                def evacuate_attended(n):
                    p, u, b, hh, _ = ph.where(n)
                    if hh == 0:
                        return
                    act.wait_ge(sem(f"{ph.name}_attended"), l * 4 * NPAIR + p * 4 + u + 1)
                    if p:
                        y = (p - 1, f"y{b}")
                        act.wait_ge(sem(f"{ph.name}_work_full{ph.bank(y)}"), l * half + ph.count(y))
                    nc.scalar.activation(oT[:, b, :], O_ps[b][:], ACT.Copy).then_inc(sem(f"{ph.name}_att_sb"), 1)

                for event in ph.first:
                    work(event)
                exponentials(0)
                for n in range(N + 2):
                    if n + 1 < N:
                        exponentials(n + 1)
                    if n < N:
                        evacuate_turned(n)
                    if ph.ends_unit(n - 1):
                        evacuate_attended(n - 1)
                    for event in ph.plan[n]:
                        work(event)

            def normed(k, g, bb):
                for b in range(B):
                    act.wait_ge(sem("xn_turned"), k * B + b + 1)
                    nc.scalar.activation(XT[:, b * T:(b + 1) * T], T_ps[b][:], ACT.Identity, bias=bb[:], scale=g[:])\
                      .then_inc(sem("xt_ready"), 1)

            act.wait_ge(sem("norm_in"), 32)
            act.wait_ge(sem("flag"), 1)
            general = act.value_load(flag[0:1, 0:1], min_val=0, max_val=1)
            with act.Fori(0, L) as l:
                normed(l * 3, norm_g, norm_b)
                with act.If(general > 0):
                    attention(SELF_ALL, l)
                with act.Else():
                    attention(SELF_LAST, l)
                normed(l * 3 + 1, norm_g, norm_b)
                attention(CROSS, l)
                act.wait_ge(sem("ff_w"), 96 * l + 96)
                normed(l * 3 + 2, pre_g, pre_b)
                for i in range(B * NF):
                    b, f = divmod(i, NF)
                    act.wait_ge(sem("hidden"), l * B * NF + i + 1)
                    nc.scalar.activation(hT[:, b, f, :], S_ps[i % 2][:], ACT.Relu, bias=b1[:, f:f + 1])\
                      .then_inc(sem("hidden_sb"), 1)
            features("C")
            token_softmax("L3")

        @block.vector
        def _(dve):
            def inv_sqrt(eps):
                nc.vector.tensor_scalar(veps[:], mv[:, :, 1], eps, None, ALU.add)
                dve.drain()
                nc.vector.tensor_scalar(newton[:].bitcast(I32), veps[:].bitcast(I32), 1, None, ALU.arith_shift_right)
                dve.drain()
                nc.vector.tensor_scalar(rstd[:].bitcast(I32), newton[:].bitcast(I32), -1.0, float(RSQRT_SEED),
                                        ALU.mult, ALU.add)
                dve.drain()
                for _ in range(NEWTON):
                    nc.vector.tensor_tensor(newton[:], rstd[:], rstd[:], ALU.mult)
                    dve.drain()
                    nc.vector.tensor_tensor(newton[:], newton[:], veps[:], ALU.mult)
                    dve.drain()
                    nc.vector.tensor_scalar(newton[:], newton[:], -0.5, 1.5, ALU.mult, ALU.add)
                    dve.drain()
                    nc.vector.tensor_tensor(rstd[:], rstd[:], newton[:], ALU.mult)
                    dve.drain()

            def layer_norm(dst, eps, done=None):
                dve.drain()
                for t in range(NT):
                    nc.vector.bn_stats(stats[:, t, :], X[:, t, :])
                dve.drain()
                for t in range(NT):
                    nc.vector.bn_aggr(mv[:, t, :], stats[:, t, :])
                dve.drain()
                inv_sqrt(eps)
                for t in range(NT):
                    last = nc.vector.tensor_scalar(dst[:, t, :], X[:, t, :], mv[:, t, 0:1], rstd[:, t:t + 1],
                                                   ALU.subtract, ALU.mult)
                    if done and t % TB == TB - 1:
                        last.then_inc(sem(done), 1)

            def outer_v(s):
                dve.wait_ge(sem("outer_in" + s), 16 * 8)
                dve.wait_ge(sem(s + "_v"), 1)
                for b in range(B):
                    last = nc.vector.tensor_tensor(vo[:, b, :], S_ps[1][:, b * P:(b + 1) * P], bv[s][:], ALU.add)
                last.then_inc(sem(s + "_v_sb"), 1)

            def token_softmax(s):
                outer_v(s)
                for b in range(B):
                    dve.wait_ge(sem(s + "_scores"), b + 1)
                    nc.vector.reduce_max(omax[0:M, b:b + 1], O_ps[b][0:M, :], AX)
                    dve.drain()
                    nc.vector.tensor_scalar(onmx[0:M, b:b + 1], omax[0:M, b:b + 1], -float(E) ** -0.5, None,
                                            ALU.mult).then_inc(sem(s + "_max"), 1)
                for b in range(B):
                    dve.wait_ge(sem(s + "_exp"), b + 1)
                    nc.vector.reciprocal(orec[0:M, b:b + 1], osum[0:M, b:b + 1])
                    dve.drain()
                    nc.vector.tensor_scalar(OP[0:M, b, :], OP[0:M, b, :], orec[0:M, b:b + 1], None, ALU.mult)\
                      .then_inc(sem(s + "_weights"), 1)
                for b in range(B):
                    dve.wait_ge(sem(s + "_pred"), b + 1)
                    rows = X[:, b * TB:(b + 1) * TB, :]
                    nc.vector.tensor_tensor(rows, tiles(W_ps[b][:]), rows, ALU.add)
                layer_norm(X, EPS_LATENT)
                dve.drain()
                for b in range(B):
                    rows = X[:, b * TB:(b + 1) * TB, :]
                    g = gam[s][:].unsqueeze(1).broadcast_to([P, TB, E])
                    nc.vector.tensor_tensor(rows, rows, g, ALU.mult)
                    dve.drain()
                    g = bet[s][:].unsqueeze(1).broadcast_to([P, TB, E])
                    nc.vector.tensor_tensor(rows, rows, g, ALU.add)\
                      .then_inc(sem("B_src" if s == "L0" else "out_ready"), 1)

            for s in range(2):
                nc.vector.memset(kz[D:P, s, 0, :], 0.0)
                nc.vector.memset(kz[0:D, s, 1, :], 0.0).then_inc(sem("kz_zero"), 1)
            dve.wait_ge(sem("mask_in"), 32)
            nc.vector.tensor_scalar(self_bias[:], mask_i[:], 0, BIG, ALU.is_equal, ALU.mult)
            dve.wait_ge(sem("consts"), 1)
            nc.vector.tensor_scalar(cross_bias[:, :, 0:M], cmask_i[:], 0, BIG, ALU.is_equal, ALU.mult)
            dve.drain()
            nc.vector.tensor_reduce(bad[:, :, 0], self_bias[:, :, 0:KEYS], AX, ALU.min)
            nc.vector.tensor_reduce(bad[:, :, 1], self_bias[:, :, KEYS:T], AX, ALU.min)
            dve.drain()
            nc.vector.tensor_scalar(bad[:, :, 0], bad[:, :, 0], 0.0, None, ALU.is_equal)
            nc.vector.tensor_scalar(bad[:, :, 1], bad[:, :, 1], 0.0, None, ALU.is_gt)
            dve.drain()
            nc.vector.tensor_reduce(badp[:], bad[:].rearrange("p t a -> p (t a)"), AX, ALU.max)\
              .then_inc(sem("bad_rows"), 1)

            dve.wait_ge(sem("x_in"), 16)
            token_softmax("L0")
            outer_v("L1")
            for b in range(B):
                dve.wait_ge(sem("L1_scores"), b + 1)
                nc.vector.tensor_reduce(omax[:, b * TB:(b + 1) * TB], tiles(O_ps[b][:])[:, :, 0:M], AX, ALU.max)
                dve.drain()
                nc.vector.tensor_scalar(onmx[:, b * TB:(b + 1) * TB], omax[:, b * TB:(b + 1) * TB],
                                        -float(E) ** -0.5, None, ALU.mult).then_inc(sem("L1_max"), 1)
            for b in range(B):
                dve.wait_ge(sem("L1_exp"), b + 1)
                nc.vector.reciprocal(orec[:, b * TB:(b + 1) * TB], osum[:, b * TB:(b + 1) * TB])
                dve.drain()
                rows = XN[:, b * TB:(b + 1) * TB, 0:M]
                nc.vector.tensor_tensor(rows, rows, orec[:, b * TB:(b + 1) * TB].unsqueeze(2).broadcast_to([P, TB, M]),
                                        ALU.mult).then_inc(sem("L1_weights"), 1)
            nc.vector.tensor_tensor(X[:], X[:], bo1[:].unsqueeze(1).broadcast_to([P, NT, E]), ALU.add)
            dve.drain()
            for b in range(B):
                dve.wait_ge(sem("L1_out"), b + 1)
                rows = X[:, b * TB:(b + 1) * TB, :]
                nc.vector.tensor_tensor(rows, tiles(W_ps[b][:]), rows, ALU.add)
            dve.drain().then_inc(sem("L1_done"), 1)
            dve.wait_ge(sem("bad_sum"), 1)
            nc.vector.tensor_scalar(flag_f[:], O_ps[0][0:1, 0:1], 1.0, None, ALU.min)
            dve.drain()
            if force_all:
                nc.vector.tensor_scalar(flag[:], flag_f[:], 0.0, 1.0, ALU.mult, ALU.add).then_inc(sem("flag"), 1)
            else:
                nc.vector.tensor_copy(flag[:], flag_f[:]).then_inc(sem("flag"), 1)

            def attention(ph, l, done):
                cross = ph is CROSS
                N, half = ph.chunks, ph.per_bank

                def work(event):
                    p, what = event
                    if what == "q0":
                        return
                    bk_ = ph.bank(event)
                    w, slot = W_ps[bk_], p % 2
                    b = int(what[1]) if what[1:] else 0
                    dve.wait_ge(sem(f"{ph.name}_work_full{bk_}"), l * half + ph.count(event))
                    if what[0] == "q":
                        last = nc.vector.tensor_scalar(qT[:, slot, b * T:(b + 1) * T], w[:], -float(D) ** -0.5, None,
                                                       ALU.mult)
                    elif what[0] == "k":
                        cols = slice(b * T, (b + 1) * T) if ph.wide else slice(0, B * P)
                        n = cols.stop - cols.start
                        nc.vector.tensor_copy(kz[0:D, slot, 0, cols], w[0:D, 0:n])
                        last = nc.vector.tensor_copy(kz[D:P, slot, 1, cols], w[D:P, 0:n])
                    elif what[0] == "v":
                        n = TB if ph.wide else B
                        last = nc.vector.tensor_copy(vv[:, slot, b * TB:b * TB + n, :], tiles(w[:])[:, 0:n, :])
                    else:
                        rows = X[:, b * TB:(b + 1) * TB, :]
                        last = nc.vector.tensor_tensor(rows, tiles(w[:]), rows, ALU.add)
                    last.then_inc(sem(f"{ph.name}_work_free{bk_}"), 1)

                def masked(n):
                    p, u, b, hh, qt = ph.where(n)
                    s = n % 2
                    for t in range(1 if ph.wide else TB):
                        w = T if ph.wide else P
                        cols = slice(t * w, (t + 1) * w)
                        if cross:
                            bias = cross_bias[:, b, :]
                        else:
                            bias = self_bias[:, b * TB + qt + t, ph.key_base:T]
                        last = nc.vector.tensor_tensor_reduce(out=Sm[:, s, cols], in0=S_ps[s][:, cols], in1=bias,
                                                              scale=1.0, scalar=3.4e38, op0=ALU.add, op1=ALU.min,
                                                              accum_out=mn[:, s, t:t + 1])
                    last.then_inc(sem(f"{ph.name}_masked"), 1)

                def reciprocals(n):
                    k = 1 if ph.wide else TB
                    if n + 1 < N:
                        dve.wait_ge(sem(f"{ph.name}_scores"), l * N + n + 2)
                    dve.wait_ge(sem(f"{ph.name}_exp"), l * N + n + 1)
                    nc.vector.reciprocal(rsum[:, n % 2, 0:k], sums[:, n % 2, 0:k]).then_inc(sem(f"{ph.name}_rsum"), 1)

                def weights(n):
                    s = n % 2
                    dve.wait_ge(sem(f"{ph.name}_rsum"), l * N + n + 1)
                    if ph.wide:
                        last = nc.vector.tensor_scalar(Pb[:, s, :], Pb[:, s, :], rsum[:, s, 0:1], None, ALU.mult)
                    else:
                        last = nc.vector.tensor_tensor(tiles(Pb[:, s, :]), tiles(Pb[:, s, :]),
                                                       rsum[:, s, :].unsqueeze(2).broadcast_to([P, TB, P]), ALU.mult)
                    last.then_inc(sem(f"{ph.name}_weights"), 1)

                for event in ph.first:
                    work(event)
                dve.wait_ge(sem(f"{ph.name}_scores"), l * N + 1)
                nc.vector.memset(carrier[:], 0.0)
                masked(0)
                for n in range(N + 2):
                    if n < N:
                        reciprocals(n)
                    if n + 1 < N:
                        masked(n + 1)
                    if n < N:
                        weights(n)
                    for event in ph.plan[n]:
                        work(event)
                dve.drain().then_inc(sem(done), 1)

            def add_row(r):
                nc.vector.tensor_tensor(X[:], X[:], r[:].unsqueeze(1).broadcast_to([P, NT, E]), ALU.add)

            dve.wait_ge(sem("kz_zero"), 2)
            dve.wait_ge(sem("flag"), 1)
            general = dve.value_load(flag[0:1, 0:1], min_val=0, max_val=1)
            with dve.Fori(0, L) as l:
                layer_norm(XN, EPS_DEC, "xn_ready")
                dve.drain()
                dve.wait_ge(sem("self_w"), 64 * l + 64)
                add_row(sob)
                with dve.If(general > 0):
                    attention(SELF_ALL, l, "self_done")
                with dve.Else():
                    attention(SELF_LAST, l, "self_done")
                layer_norm(XN, EPS_DEC, "xn_ready")
                dve.drain()
                dve.wait_ge(sem("cross_w"), 64 * l + 64)
                add_row(cob)
                attention(CROSS, l, "cross_done")
                layer_norm(XN, EPS_DEC, "xn_ready")
                dve.drain()
                dve.wait_ge(sem("ff_w"), 96 * l + 96)
                add_row(b2)
                dve.drain()
                for b in range(B):
                    dve.wait_ge(sem("ff_out"), l * B + b + 1)
                    rows = X[:, b * TB:(b + 1) * TB, :]
                    nc.vector.tensor_tensor(rows, tiles(O_ps[b][:]), rows, ALU.add)
                dve.drain().then_inc(sem("ff_done"), 1)
            dve.drain().then_inc(sem("C_src"), 2)
            token_softmax("L3")


_OUT_SHAPE = (2, 512, 128)


def kernel(**inputs):
    import numpy as _np
    import concourse.bacc as _bacc
    from concourse import mybir as _mybir
    from concourse.bass_utils import run_bass_kernel_spmd as _run

    nc = _bacc.Bacc("TRN2", target_bir_lowering=False, num_devices=1)
    arrays, args = {}, {}
    for name, value in inputs.items():
        v = _np.ascontiguousarray(value)
        arrays[f"in_{name}"] = v
        args[name] = nc.dram_tensor(f"in_{name}", v.shape, _mybir.dt.from_np(v.dtype), kind="ExternalInput").ap()
    out = nc.dram_tensor("out_x", _OUT_SHAPE, _mybir.dt.float32, kind="ExternalOutput").ap()
    build(nc, args, out)
    r = _run(nc, [arrays], core_ids=[0])
    return r.results[0]["out_x"]
```

```python
from contextlib import ExitStack

import concourse.bass as bass
from concourse import mybir

F32 = mybir.dt.float32
I32 = mybir.dt.int32
ALU = mybir.AluOpType
ACT = mybir.ActivationFunctionType
AX = mybir.AxisListType.X

B, T, E = 2, 512, 128
M, CD = 77, 64
L, H, D, FF = 6, 16, 64, 512
P = 128
NT = B * T // P
TB = T // P
NPAIR = H * D // P
NF = FF // P
KEYS = T - P
BIG = 1.0e30
PAD = 3.0e38
EPS_LATENT, EPS_DEC = 1e-6, 1e-5
RSQRT_SEED = 0x5F3759DF
NEWTON = 3


class Ring:

    def __init__(self, name, order):
        self.name = name
        self.index = {e: i for i, e in enumerate(order)}
        self.total = [(len(order) + 1) // 2, len(order) // 2]
        assert len(self.index) == len(order)

    def bank(self, event):
        return self.index[event] % 2

    def count(self, event):
        return self.index[event] // 2 + 1

    def full(self, event):
        return f"{self.name}_work_full{self.bank(event)}"

    def free(self, event):
        return f"{self.name}_work_free{self.bank(event)}"

    def value(self, event, l):
        return l * self.total[self.bank(event)] + self.count(event)


FOLD = [(k, i) for k in ("tq", "tk", "tv") for i in (0, 1)] + [(k, i) for k in ("m", "n") for i in range(4)]


class Stream:

    def __init__(self, name, wide, cross):
        self.name, self.wide, self.cross = name, wide, cross
        self.groups = H if wide else H // TB
        self.heads = 1 if wide else TB
        self.per_batch = self.groups * TB
        self.chunks = B * self.per_batch
        self.key_base = 0 if wide else KEYS
        self.first = [("G", 0), ("G", 1)]
        self.plan = [[] for _ in range(self.chunks + TB)]
        self.norm = [[] for _ in range(self.chunks + TB)]
        second = self.per_batch
        if cross:
            self.normalise(0, 1, fin=True)
        else:
            self.normalise(0, 1, fin=False)
        self.normalise(second + TB, 0, fin=True)
        for g in range(B * self.groups):
            if g > 1:
                self.plan[TB * g - 6].append(("G", g))
            self.plan[TB * g].append(("V", g))
        if not cross:
            for i, e in enumerate(FOLD):
                self.plan[2 + i].append(e)
        self.ring = Ring(name, self.first + [e for step in self.plan for e in step])

    def normalise(self, at, b, fin):
        if fin:
            self.plan[at].append(("fin", b))
        for k in range(5):
            self.norm[at + k].append((b, k))
        self.plan[at + 5].append(("xn", b))

    def where(self, n):
        g, qt = divmod(n, TB)
        return g, qt, g // self.groups, g % self.groups


SELF_ALL = Stream("self_all", True, False)
SELF_LAST = Stream("self_last", False, False)
CROSS = Stream("cross", False, True)
TOP = Ring("top", FOLD + [("xn", 0)])
FFN = Ring("ffn", [("fin", 1), ("xn", 1)])


vector_empties = {(s.ring.name, e) for s in (SELF_ALL, SELF_LAST, CROSS) for e in s.ring.index
                  if e[0] in ("V", "fin", "n")} | {("ffn", ("fin", 1))}
out_index = {("self_all", 0): 0, ("self_last", 0): 0, ("cross", 1): 1, ("cross", 0): 2, ("ffn", 1): 3}
xn_index = {("top", 0): 0, ("self_all", 1): 1, ("self_last", 1): 1, ("self_all", 0): 2, ("self_last", 0): 2,
            ("cross", 1): 3, ("cross", 0): 4, ("ffn", 1): 5}
SELF_W = 16 * 5


def build(nc, a, out, force_all=False):
    with ExitStack() as ctx:
        def sb(name, shape, dt=F32):
            return ctx.enter_context(nc.sbuf_tensor(name, shape, dt))

        sems = {}

        def sem(name):
            if name not in sems:
                sems[name] = ctx.enter_context(nc.semaphore(name))
            return sems[name]

        ident = sb("ident", [P, P])
        ones = sb("ones", [P, 1])
        X = sb("X", [P, NT, E])
        XN = sb("XN", [P, NT, E])
        XT = sb("XT", [P, B * T])
        ctx_in = sb("ctx_in", [P, B, CD])
        ctxT = sb("ctxT", [P, B, P])
        self_bias = sb("self_bias", [P, NT, T])
        cmask_i = sb("cmask_i", [P, B, M], I32)
        cross_bias = sb("cross_bias", [P, B, P])
        stats = sb("stats", [P, NT, 6])
        mv = sb("mv", [P, NT, 2])
        veps = sb("veps", [P, NT])
        rstd = sb("rstd", [P, NT])
        newton = sb("newton", [P, NT])
        qT = sb("qT", [P, B * T])
        oT = sb("oT", [P, B, T])
        wqT = sb("wqT", [P, NPAIR, 2, E])
        wkT = sb("wkT", [P, NPAIR, E])
        wvT = sb("wvT", [P, NPAIR, E])
        Ms, Mc = sb("Ms", [P, H, E]), sb("Mc", [P, H, E])
        Ns, Nc = sb("Ns", [P, H, E]), sb("Nc", [P, H, E])
        G = sb("G", [P, 2, T])
        V = sb("V", [P, 2, TB, E])
        Sm = sb("Sm", [P, 2, T])
        Pb = sb("Pb", [P, 2, T])
        PT = sb("PT", [P, 2, TB, T])
        mn = sb("mn", [P, 2, TB])
        sums = sb("sums", [P, 2, TB])
        rsum = sb("rsum", [P, 2, TB])
        hT = sb("hT", [P, B, NF, T])
        saq, sakv = sb("saq", [P, H * D]), sb("sakv", [P, 2 * H * D])
        saow = sb("saow", [P, NPAIR, 2, E])
        caq, cakv = sb("caq", [P, H * D]), sb("cakv", [P, 2 * H * D])
        caow = sb("caow", [P, NPAIR, 2, E])
        w1, w2 = sb("w1", [P, FF]), sb("w2", [P, NF, E])
        sob, cob, b2 = sb("sob", [P, E]), sb("cob", [P, E]), sb("b2", [P, E])
        b1 = sb("b1", [P, NF])
        pre_g, pre_b = sb("pre_g", [P, 1]), sb("pre_b", [P, 1])
        norm_g, norm_b = sb("norm_g", [P, 1]), sb("norm_b", [P, 1])
        OUTER = ["L0", "L1", "L3"]
        wq = {s: sb(f"{s}wq", [P, P]) for s in OUTER}
        wk = {s: sb(f"{s}wk", [CD, P]) for s in OUTER}
        wv = {s: sb(f"{s}wv", [CD, P]) for s in OUTER}
        bq = {s: sb(f"{s}bq", [P, 1]) for s in OUTER}
        bk = {s: sb(f"{s}bk", [P, 1]) for s in OUTER}
        bv = {s: sb(f"{s}bv", [P, P]) for s in OUTER}
        gam = {s: sb(f"{s}gam", [P, P]) for s in ("L0", "L3")}
        bet = {s: sb(f"{s}bet", [P, P]) for s in ("L0", "L3")}
        wo1, bo1 = sb("wo1", [P, P]), sb("bo1", [P, P])
        kT = sb("kT", [P, B, P])
        vo = sb("vo", [P, B, P])
        omax = sb("omax", [P, NT])
        onmx = sb("onmx", [P, NT])
        osum = sb("osum", [P, NT])
        orec = sb("orec", [P, NT])
        OP = sb("OP", [P, B, T])
        carrier = sb("carrier", [P, 4])
        bad = sb("bad", [P, NT, 2])
        badp = sb("badp", [P, 1])
        flag_f = sb("flag_f", [1, 1])
        flag = sb("flag", [1, 1], I32)

        def bank(name):
            return ctx.enter_context(nc.psum_tensor(name, [P, T], F32))

        S_ps = [bank("S0"), bank("S1")]
        T_ps = [bank("T0"), bank("T1")]
        O_ps = [bank("O0"), bank("O1")]
        W_ps = [bank("W0"), bank("W1")]

        def tiles(ap):
            return ap.rearrange("p (t e) -> p t e", e=P)

        def row(v):
            return v.rearrange("(a n) -> a n", a=1).broadcast_to([P, v.shape[0]])

        def col(v):
            return v.rearrange("(p a) -> p a", a=1)

        block = ctx.enter_context(nc.Block())

        @block.sync
        def _(sp):
            sp.dma_start(X[:], a["x"].rearrange("b (t p) e -> p (b t) e", p=P)).then_inc(sem("x_in"), 16)
            for b in range(B):
                sp.dma_start(ctx_in[0:M, b, :], a["ctx_512"][b]).then_inc(sem("ctx_in"), 16)
            for s in OUTER:
                w = f"{s}_xattn_"
                for dst, src in ((wq[s][:], a[w + "Wq"]), (wk[s][:], a[w + "Wk"]), (wv[s][:], a[w + "Wv"]),
                                 (bq[s][:], col(a[w + "bq"])), (bk[s][:], col(a[w + "bk"])),
                                 (bv[s][:], row(a[w + "bv"]))):
                    sp.dma_start(dst, src).then_inc(sem("outer_in" + s), 16)
                if s == "L1":
                    sp.dma_start(wo1[:], a[w + "Wo"]).then_inc(sem("outer_inL1"), 16)
                    sp.dma_start(bo1[:], row(a[w + "bo"])).then_inc(sem("outer_inL1"), 16)
                else:
                    sp.dma_start(gam[s][:], row(a[w + "gamma"])).then_inc(sem("outer_in" + s), 16)
                    sp.dma_start(bet[s][:], row(a[w + "beta"])).then_inc(sem("outer_in" + s), 16)
                if s == "L0":
                    sp.dma_start(self_bias[:].bitcast(I32), a["mask_BxSxS_ik0"].rearrange("b (t p) k -> p (b t) k", p=P))\
                      .then_inc(sem("mask_in"), 16)
                    sp.dma_start(cmask_i[:], a["mask_Bx1xS2_if1"].rearrange("b a m -> a b m").broadcast_to([P, B, M]))\
                      .then_inc(sem("mask_in"), 16)
                    sp.dma_start(norm_g[:], col(a["L2_xattn_norm_g"])).then_inc(sem("norm_in"), 16)
                    sp.dma_start(norm_b[:], col(a["L2_xattn_norm_b"])).then_inc(sem("norm_in"), 16)

            def layer(name, l):
                v = a["L2_xattn_" + name]
                v = v[bass.ds(l, 1)]
                return v.rearrange("a p n -> p (a n)") if len(v.shape) == 3 else v

            def heads(name, l):
                return a["L2_xattn_" + name][bass.ds(l, 1)].rearrange("a (g p) n -> p (a g) n", p=P)

            def load_self(l):
                for dst, src in ((saq[:], layer("sa_q", l)), (sakv[:], layer("sa_kv", l)),
                                 (saow[0:D, :, 0, :], heads("sa_ow", l)[0:D]), (saow[D:P, :, 1, :], heads("sa_ow", l)[D:P]),
                                 (sob[:], layer("sa_ob", l).broadcast_to([P, E]))):
                    sp.dma_start(dst, src).then_inc(sem("self_w"), 16)

            def load_cross(l):
                for dst, src in ((caq[:], layer("ca_q", l)), (cakv[0:CD, :], layer("ca_kv", l)),
                                 (caow[0:D, :, 0, :], heads("ca_ow", l)[0:D]), (caow[D:P, :, 1, :], heads("ca_ow", l)[D:P]),
                                 (cob[:], layer("ca_ob", l).broadcast_to([P, E]))):
                    sp.dma_start(dst, src).then_inc(sem("cross_w"), 16)

            def load_ff(l):
                for dst, src in ((w1[:], layer("ff_w1", l)),
                                 (w2[:], a["L2_xattn_ff_w2"][bass.ds(l, 1)].rearrange("a (g p) n -> p (a g) n", p=P)),
                                 (b2[:], layer("ff_b2", l).broadcast_to([P, E])),
                                 (b1[:], layer("ff_b1", l).rearrange("a (g p) -> p (a g)", p=P)),
                                 (pre_g[:], layer("pre_g", l).rearrange("a p -> p a")),
                                 (pre_b[:], layer("pre_b", l).rearrange("a p -> p a"))):
                    sp.dma_start(dst, src, allow_slow_non_contiguous=True).then_inc(sem("ff_w"), 16)

            sp.wait_ge(sem("pads_zero"), 1)
            load_self(0)
            load_cross(0)
            load_ff(0)
            with sp.Fori(0, L - 1) as l:
                sp.wait_ge(sem("out_sum"), 4 * l + 1)
                load_self(l + 1)
                sp.wait_ge(sem("out_sum"), 4 * l + 3)
                load_cross(l + 1)
                sp.wait_ge(sem("ff_done"), l + 1)
                load_ff(l + 1)
            for b in range(B):
                sp.wait_ge(sem("out_ready"), b + 1)
                sp.dma_start(out[b].rearrange("(t p) e -> p t e", p=P), X[:, b * TB:(b + 1) * TB, :])\
                  .then_inc(sem("out_done"), 16)
            sp.wait_ge(sem("out_done"), 32)

        @block.gpsimd
        def _(gp):
            nc.gpsimd.memset(saow[D:P, :, 0, :], 0.0).then_inc(sem("gp_pad"), 1)
            nc.gpsimd.memset(saow[0:D, :, 1, :], 0.0).then_inc(sem("gp_pad"), 1)
            nc.gpsimd.memset(caow[D:P, :, 0, :], 0.0).then_inc(sem("gp_pad"), 1)
            nc.gpsimd.memset(caow[0:D, :, 1, :], 0.0).then_inc(sem("gp_pad"), 1)
            nc.gpsimd.memset(cakv[CD:P, :], 0.0).then_inc(sem("gp_pad"), 1)
            nc.gpsimd.memset(wqT[D:P, :, 0, :], 0.0).then_inc(sem("gp_pad"), 1)
            nc.gpsimd.memset(wqT[0:D, :, 1, :], 0.0).then_inc(sem("gp_pad"), 1)
            gp.wait_ge(sem("gp_pad"), 7)
            nc.gpsimd.memset(ident[:], 0.0).then_inc(sem("gp_zero"), 1)
            nc.gpsimd.memset(ones[:], 1.0).then_inc(sem("gp_zero"), 1)
            nc.gpsimd.memset(ctxT[:], 0.0).then_inc(sem("gp_zero"), 1)
            nc.gpsimd.memset(cross_bias[:], PAD).then_inc(sem("gp_zero"), 1)
            gp.wait_ge(sem("gp_zero"), 4)
            nc.gpsimd.affine_select(out=ident[:], in_=ident[:], compare_op=ALU.not_equal, fill=1.0, base=0,
                                    pattern=[[-1, P]], channel_multiplier=1).then_inc(sem("consts"), 1)
            gp.wait_ge(sem("consts"), 1)
            nc.gpsimd.memset(carrier[:], 0.0).then_inc(sem("pads_zero"), 1)

        @block.tensor
        def _(pe):
            def transposes(src, bank, n, name):
                for t in range(TB):
                    last = nc.tensor.transpose(bank[:, t * P:(t + 1) * P], src[:, n * TB + t, :], ident[:])
                last.then_inc(sem(name), 1)

            def to_features(src, name):
                for b in range(B):
                    pe.wait_ge(sem(name + "_src"), b + 1)
                    transposes(src, T_ps[b], b, name + "_turned")

            def outer_projections(s, full, nb):
                pe.wait_ge(sem("outer_in" + s), 16 * 8)
                for b in range(B):
                    pe.wait_ge(sem(nb + "_xt"), b + 1)
                    nc.tensor.matmul(W_ps[b][:], wq[s][:], XT[:, b * T:(b + 1) * T], start=True, stop=True)\
                      .then_inc(sem(s + "_q"), 1)
                nc.tensor.matmul(S_ps[0][:, 0:B * P], wk[s][:], ctxT[0:CD].rearrange("c b m -> c (b m)"),
                                 start=True, stop=True).then_inc(sem(s + "_k"), 1)
                for b in range(B):
                    last = nc.tensor.matmul(S_ps[1][:, b * P:(b + 1) * P], ctxT[0:CD, b, :], wv[s][:],
                                            start=True, stop=True)
                last.then_inc(sem(s + "_v"), 1)

            def token_softmax(s, nb):
                outer_projections(s, None, nb)
                for b in range(B):
                    pe.wait_ge(sem(s + "_qk_sb"), 3 + 0 * b)
                    nc.tensor.matmul(O_ps[b][0:M, :], kT[:, b, 0:M], qT[:, b * T:(b + 1) * T],
                                     start=True, stop=True).then_inc(sem(s + "_scores"), 1)
                for b in range(B):
                    pe.wait_ge(sem(s + "_weights"), b + 1)
                    pe.wait_ge(sem(s + "_v_sb"), 1)
                    for t in range(TB):
                        last = nc.tensor.matmul(W_ps[b][:, t * P:(t + 1) * P], OP[0:M, b, t * P:(t + 1) * P],
                                                vo[0:M, b, :], start=True, stop=True)
                    last.then_inc(sem(s + "_pred"), 1)

            pe.wait_ge(sem("consts"), 1)
            pe.wait_ge(sem("ctx_in"), 16 * B)
            for b in range(B):
                last = nc.tensor.transpose(S_ps[0][0:CD, b * P:b * P + M], ctx_in[0:M, b, :], ident[0:M, 0:M])
            last.then_inc(sem("ctx_turned"), 1)
            pe.wait_ge(sem("x_in"), 16)
            for b in range(B):
                transposes(X, T_ps[b], b, "A_turned")
            pe.wait_ge(sem("ctx_sb"), 1)
            token_softmax("L0", "A")
            to_features(X, "B")
            outer_projections("L1", None, "B")
            pe.wait_ge(sem("L1_qk_sb"), 3)
            for b in range(B):
                for t in range(TB):
                    last = nc.tensor.matmul(O_ps[b][:, t * P:t * P + M],
                                            qT[:, (b * TB + t) * P:(b * TB + t + 1) * P], kT[:, b, 0:M],
                                            start=True, stop=True)
                last.then_inc(sem("L1_scores"), 1)
            for b in range(B):
                pe.wait_ge(sem("L1_weights"), b + 1)
                for t in range(TB):
                    last = nc.tensor.transpose(T_ps[b][0:M, t * P:(t + 1) * P], XN[:, b * TB + t, 0:M], ident[:])
                last.then_inc(sem("L1_turned"), 1)
            pe.wait_ge(sem("L1_v_sb"), 1)
            for b in range(B):
                pe.wait_ge(sem("L1_wT"), b + 1)
                nc.tensor.matmul(S_ps[b][:], vo[0:M, b, :], OP[0:M, b, :], start=True, stop=True)\
                  .then_inc(sem("L1_att"), 1)
            for b in range(B):
                pe.wait_ge(sem("L1_att_sb"), b + 1)
                for t in range(TB):
                    last = nc.tensor.matmul(W_ps[b][:, t * P:(t + 1) * P], oT[:, b, t * P:(t + 1) * P], wo1[:],
                                            start=True, stop=True)
                last.then_inc(sem("L1_out"), 1)
            pe.wait_ge(sem("bad_rows"), 1)
            pe.wait_ge(sem("L1_done"), 1)
            nc.tensor.matmul(O_ps[0][0:1, 0:1], badp[:], ones[:], start=True, stop=True).then_inc(sem("bad_sum"), 1)

            def read(ring, events, l, to_fill=None):
                need = [0, 0]
                for e in events:
                    need[ring.bank(e)] = max(need[ring.bank(e)], ring.count(e))
                if to_fill is not None:
                    k = ring.bank(to_fill)
                    need[k] = max(need[k], ring.count(to_fill) - 1)
                for k in range(2):
                    if need[k]:
                        pe.wait_ge(sem(f"{ring.name}_work_free{k}"), l * ring.total[k] + need[k])

            def pair_tiles(w, i):
                return [(j, w[:, (i * TB + j) * P:(i * TB + j + 1) * P]) for j in range(TB)]

            def work(ring, event, l, q, kv, ow, M, N, st=None):
                what, i = event
                w = W_ps[ring.bank(event)]
                before = []
                if event == ("m", 0):
                    before = [(k, j) for k in ("tq", "tk") for j in range(2)]
                elif event == ("n", 0):
                    before = [("tv", 0), ("tv", 1)]
                elif what == "G" and i == st.groups and not st.cross:
                    before = [("xn", 1)]
                read(ring, before, l, to_fill=event)
                if what in ("tq", "tk", "tv"):
                    src = {"tq": q, "tk": kv, "tv": kv[:, H * D:]}[what]
                    for j, cols in pair_tiles(src, i):
                        last = nc.tensor.transpose(w[:, j * P:(j + 1) * P], cols, ident[:])
                elif what in ("m", "n"):
                    for j in range(2):
                        p = 2 * i + j
                        lhs, rhs = (wkT, wqT) if what == "m" else (wvT, ow)
                        last = nc.tensor.matmul(w[:, j * 2 * E:(j + 1) * 2 * E], lhs[:, p, :],
                                                rhs[:, p, :, :].rearrange("p h e -> p (h e)"), start=True, stop=True)
                elif what == "G":
                    b, g = divmod(i, st.groups)
                    if st.wide:
                        last = nc.tensor.matmul(w[:], M[:, g, :], XT[:, b * T:(b + 1) * T], start=True, stop=True)
                    else:
                        keys = ctxT[:, b, :] if st.cross else XT[:, b * T + KEYS:(b + 1) * T]
                        for j in range(TB):
                            last = nc.tensor.matmul(w[:, j * P:(j + 1) * P], M[:, g * TB + j, :], keys,
                                                    start=True, stop=True)
                elif what == "V":
                    b, g = divmod(i, st.groups)
                    if st.wide:
                        for j in range(TB):
                            last = nc.tensor.matmul(w[:, j * P:(j + 1) * P],
                                                    XT[:, b * T + j * P:b * T + (j + 1) * P], N[:, g, :],
                                                    start=True, stop=True)
                    else:
                        keys = ctxT[:, b, :] if st.cross else XT[:, b * T + KEYS:(b + 1) * T]
                        last = nc.tensor.matmul(w[:], keys, N[:, g * TB:(g + 1) * TB, :].rearrange("p h e -> p (h e)"),
                                                start=True, stop=True)
                elif what == "fin":
                    pe.wait_ge(sem("oT_sb"), l * 2 * B + out_index[ring.name, i] + 1)
                    for t in range(TB):
                        last = nc.tensor.transpose(w[:, t * P:(t + 1) * P], oT[:, i, t * P:(t + 1) * P], ident[:])
                else:
                    pe.wait_ge(sem("xn_ready"), l * 3 * B + xn_index[ring.name, i] + 1)
                    for t in range(TB):
                        last = nc.tensor.transpose(w[:, t * P:(t + 1) * P], XN[:, i * TB + t, :], ident[:])
                last.then_inc(sem(ring.full(event)), 1)

            def all_read(ring, l):
                for k in range(2):
                    pe.wait_ge(sem(f"{ring.name}_work_free{k}"), l * ring.total[k] + ring.total[k])

            def attention(st, l):
                C, ring = st.chunks, st.ring
                M, N = (Mc, Nc) if st.cross else (Ms, Ns)

                def do(event):
                    work(ring, event, l, caq, cakv, caow, M, N, st)

                def scores(n):
                    g, qt, b, _ = st.where(n)
                    if qt == 0:
                        read(ring, [("G", g)] + [("xn", 1)] * (n == st.per_batch), l)
                    if n >= 2:
                        pe.wait_ge(sem(f"{st.name}_masked"), l * C + n - 1)
                    nc.tensor.matmul(S_ps[n % 2][:], XT[:, (b * TB + qt) * P:(b * TB + qt + 1) * P], G[:, g % 2, :],
                                     start=True, stop=True).then_inc(sem(f"{st.name}_scores"), 1)

                def turn(n):
                    pe.wait_ge(sem(f"{st.name}_weights"), l * C + n + 1)
                    if n >= 2:
                        pe.wait_ge(sem(f"{st.name}_turned_sb"), l * C + n - 1)
                    for t in range(TB):
                        last = nc.tensor.transpose(T_ps[n % 2][:, t * P:(t + 1) * P],
                                                   Pb[:, n % 2, t * P:(t + 1) * P], ident[:])
                    last.then_inc(sem(f"{st.name}_turned"), 1)

                def attend(n):
                    g, blk = n // TB - 1, n % TB
                    b, gb = divmod(g, st.groups)
                    if blk == 0:
                        pe.wait_ge(sem(f"{st.name}_turned_sb"), l * C + (g + 1) * TB)
                        read(ring, [("V", g)], l)
                    last_of_batch = gb == st.groups - 1 and blk == TB - 1
                    last = nc.tensor.matmul(O_ps[b][:], V[:, g % 2, blk, :], PT[:, g % 2, blk, :],
                                            start=(gb == 0 and blk == 0), stop=last_of_batch)
                    last.then_inc(sem("out_sum" if last_of_batch else f"{st.name}_attended"), 1)

                for event in st.first:
                    do(event)
                for n in range(3):
                    scores(n)
                for n in range(C + TB):
                    if n + 3 < C:
                        scores(n + 3)
                    if n >= TB:
                        attend(n)
                    if n < C:
                        turn(n)
                    for event in st.plan[n]:
                        do(event)
                all_read(ring, l)

            pe.wait_ge(sem("pads_zero"), 1)
            pe.wait_ge(sem("flag"), 1)
            general = pe.value_load(flag[0:1, 0:1], min_val=0, max_val=1)
            with pe.Fori(0, L) as l:
                pe.wait_ge(sem("self_w"), SELF_W * l + SELF_W)
                for event in TOP.index:
                    work(TOP, event, l, saq, sakv, saow, Ms, Ns)
                all_read(TOP, l)
                pe.wait_ge(sem("cross_w"), SELF_W * l + SELF_W)
                with pe.If(general > 0):
                    attention(SELF_ALL, l)
                with pe.Else():
                    attention(SELF_LAST, l)
                attention(CROSS, l)
                pe.wait_ge(sem("ff_w"), 96 * l + 96)

                def hidden(b, f):
                    i = b * NF + f
                    if i >= 2:
                        pe.wait_ge(sem("hidden_sb"), l * B * NF + i - 1)
                    nc.tensor.matmul(S_ps[i % 2][:], w1[:, f * P:(f + 1) * P], XT[:, b * T:(b + 1) * T],
                                     start=True, stop=True).then_inc(sem("hidden"), 1)

                def ff_out(b):
                    pe.wait_ge(sem("hidden_sb"), l * B * NF + (b + 1) * NF)
                    for t in range(TB):
                        for f in range(NF):
                            last = nc.tensor.matmul(T_ps[b][:, t * P:(t + 1) * P], hT[:, b, f, t * P:(t + 1) * P],
                                                    w2[:, f, :], start=(f == 0), stop=(f == NF - 1))
                    last.then_inc(sem("ff_out"), 1)

                hidden(0, 0)
                work(FFN, ("fin", 1), l, None, None, None, None, None)
                for f in range(1, NF):
                    hidden(0, f)
                ff_out(0)
                work(FFN, ("xn", 1), l, None, None, None, None, None)
                read(FFN, [("xn", 1)], l)
                for f in range(NF):
                    hidden(1, f)
                ff_out(1)
            to_features(X, "C")
            token_softmax("L3", "C")

        @block.scalar
        def _(act):
            def features(name, bias=None):
                for b in range(B):
                    act.wait_ge(sem(name + "_turned"), b + 1)
                    nc.scalar.activation(XT[:, b * T:(b + 1) * T], T_ps[b][:], ACT.Copy).then_inc(sem(name + "_xt"), 1)

            def outer_evacuations(s):
                act.wait_ge(sem("outer_in" + s), 16 * 8)
                for b in range(B):
                    act.wait_ge(sem(s + "_q"), b + 1)
                    nc.scalar.activation(qT[:, b * T:(b + 1) * T], W_ps[b][:], ACT.Identity, bias=bq[s][:])\
                      .then_inc(sem(s + "_qk_sb"), 1)
                act.wait_ge(sem(s + "_k"), 1)
                nc.scalar.activation(kT[:].rearrange("p b m -> p (b m)"), S_ps[0][:, 0:B * P], ACT.Identity,
                                     bias=bk[s][:]).then_inc(sem(s + "_qk_sb"), 1)

            act.wait_ge(sem("ctx_turned"), 1)
            act.wait_ge(sem("consts"), 1)
            nc.scalar.activation(ctxT[0:CD, :, 0:M], S_ps[0][0:CD, 0:B * P].rearrange("c (b m) -> c b m", b=B)[:, :, 0:M],
                                 ACT.Copy).then_inc(sem("ctx_sb"), 1)

            def token_softmax(s):
                outer_evacuations(s)
                for b in range(B):
                    act.wait_ge(sem(s + "_max"), b + 1)
                    nc.scalar.activation(OP[0:M, b, :], O_ps[b][0:M, :], ACT.Exp, bias=onmx[0:M, b:b + 1],
                                         scale=float(E) ** -0.5, accum_out=osum[0:M, b:b + 1])\
                      .then_inc(sem(s + "_exp"), 1)

            features("A")
            token_softmax("L0")
            features("B")
            outer_evacuations("L1")
            for b in range(B):
                act.wait_ge(sem("L1_max"), b + 1)
                for t in range(TB):
                    i = b * TB + t
                    last = nc.scalar.activation(XN[:, i, 0:M], O_ps[b][:, t * P:t * P + M], ACT.Exp,
                                                bias=onmx[:, i:i + 1], scale=float(E) ** -0.5,
                                                accum_out=osum[:, i:i + 1])
                last.then_inc(sem("L1_exp"), 1)
            for b in range(B):
                act.wait_ge(sem("L1_turned"), b + 1)
                nc.scalar.activation(OP[0:M, b, :], T_ps[b][0:M, :], ACT.Copy).then_inc(sem("L1_wT"), 1)
            for b in range(B):
                act.wait_ge(sem("L1_att"), b + 1)
                nc.scalar.activation(oT[:, b, :], S_ps[b][:], ACT.Copy).then_inc(sem("L1_att_sb"), 1)

            def work(ring, event, l, M, N):
                what, i = event
                if (ring.name, event) in vector_empties:
                    return
                w = W_ps[ring.bank(event)]
                act.wait_ge(sem(ring.full(event)), ring.value(event, l))
                rows = slice(i * TB, (i + 1) * TB)
                if what == "tq":
                    for h, half in enumerate((slice(0, D), slice(D, P))):
                        last = nc.scalar.activation(wqT[half, rows, h, :], tiles(w[half, :]), ACT.Copy,
                                                    scale=-float(D) ** -0.5)
                elif what in ("tk", "tv"):
                    last = nc.scalar.activation((wkT if what == "tk" else wvT)[:, rows, :], tiles(w[:]), ACT.Copy)
                elif what in ("m", "n"):
                    last = nc.scalar.activation((M if what == "m" else N)[:, rows, :], tiles(w[:]), ACT.Copy)
                elif what == "G":
                    last = nc.scalar.activation(G[:, i % 2, :], w[:], ACT.Copy)
                else:
                    g, bb = affine[ring.name, i]
                    last = nc.scalar.activation(XT[:, i * T:(i + 1) * T], w[:], ACT.Identity, bias=bb[:], scale=g[:])
                last.then_inc(sem(ring.free(event)), 1)

            def attention(st, l):
                C, ring = st.chunks, st.ring

                def exponentials(n):
                    act.wait_ge(sem(f"{st.name}_masked"), l * C + n + 1)
                    if n >= 2:
                        act.wait_ge(sem(f"{st.name}_turned"), l * C + n - 1)
                    s = n % 2
                    w = T if st.wide else P
                    for t in range(T // w):
                        last = nc.scalar.activation(Pb[:, s, t * w:(t + 1) * w], Sm[:, s, t * w:(t + 1) * w], ACT.Exp,
                                                    bias=mn[:, s, t:t + 1], scale=-1.0, accum_out=sums[:, s, t:t + 1])
                    last.then_inc(sem(f"{st.name}_exp"), 1)

                def evacuate_turned(n):
                    gr, qt, _, _ = st.where(n)
                    act.wait_ge(sem(f"{st.name}_turned"), l * C + n + 1)
                    if gr >= 2 and qt == 0:
                        k = TB * (gr - 1)
                        if k > st.per_batch:
                            k -= 1
                        elif k == st.per_batch:
                            act.wait_ge(sem("out_sum"), l * 2 * B + (2 if st.cross else 0) + 1)
                            k -= 1
                        act.wait_ge(sem(f"{st.name}_attended"), l * (C - B) + k)
                    nc.scalar.activation(PT[:, gr % 2, :, qt * P:(qt + 1) * P], tiles(T_ps[n % 2][:]), ACT.Copy)\
                      .then_inc(sem(f"{st.name}_turned_sb"), 1)

                for event in st.first:
                    work(ring, event, l, Mc, Nc)
                exponentials(0)
                for n in range(C + TB):
                    if n + 1 < C:
                        exponentials(n + 1)
                    if n < C:
                        evacuate_turned(n)
                    if (n + 1 - TB) % st.per_batch == 0 and n >= TB:
                        b = (n + 1 - TB) // st.per_batch - 1
                        act.wait_ge(sem("out_sum"), l * 2 * B + (2 if st.cross else 0) + b + 1)
                        nc.scalar.activation(oT[:, b, :], O_ps[b][:], ACT.Copy).then_inc(sem("oT_sb"), 1)
                    for event in st.plan[n]:
                        work(ring, event, l, Mc, Nc)

            affine = {k: (norm_g, norm_b) for k in xn_index}
            affine["cross", 0] = affine["ffn", 1] = (pre_g, pre_b)
            act.wait_ge(sem("norm_in"), 32)
            act.wait_ge(sem("pads_zero"), 1)
            act.wait_ge(sem("flag"), 1)
            general = act.value_load(flag[0:1, 0:1], min_val=0, max_val=1)
            with act.Fori(0, L) as l:
                for event in TOP.index:
                    work(TOP, event, l, Ms, Ns)
                with act.If(general > 0):
                    attention(SELF_ALL, l)
                with act.Else():
                    attention(SELF_LAST, l)
                act.wait_ge(sem("ff_w"), 96 * l + 96)
                attention(CROSS, l)

                def relu(b):
                    for f in range(NF):
                        i = b * NF + f
                        act.wait_ge(sem("hidden"), l * B * NF + i + 1)
                        nc.scalar.activation(hT[:, b, f, :], S_ps[i % 2][:], ACT.Relu, bias=b1[:, f:f + 1])\
                          .then_inc(sem("hidden_sb"), 1)

                relu(0)
                work(FFN, ("xn", 1), l, None, None)
                relu(1)
            features("C")
            token_softmax("L3")

        @block.vector
        def _(dve):
            def normalise(step, ts, dst, eps, done=None):
                v, r, w = veps[:, ts], rstd[:, ts], newton[:, ts]
                n = range(ts.start, ts.stop)
                if step == 0:
                    dve.drain()
                    for t in n:
                        nc.vector.bn_stats(stats[:, t, :], X[:, t, :])
                elif step == 1:
                    dve.drain()
                    for t in n:
                        nc.vector.bn_aggr(mv[:, t, :], stats[:, t, :])
                    dve.drain()
                    nc.vector.tensor_scalar(v, mv[:, ts, 1], eps, None, ALU.add)
                    dve.drain()
                    nc.vector.tensor_scalar(w.bitcast(I32), v.bitcast(I32), 1, None, ALU.arith_shift_right)
                    dve.drain()
                    nc.vector.tensor_scalar(r.bitcast(I32), w.bitcast(I32), -1.0, float(RSQRT_SEED), ALU.mult, ALU.add)
                    nc.vector.tensor_scalar(v, v, -0.5, None, ALU.mult)
                elif step == 2:
                    for _ in range(NEWTON):
                        dve.drain()
                        nc.vector.tensor_tensor(w, r, r, ALU.mult)
                        dve.drain()
                        nc.vector.tensor_tensor(w, w, v, ALU.mult)
                        dve.drain()
                        nc.vector.scalar_tensor_tensor(out=r, in0=w, scalar=1.5, in1=r, op0=ALU.add, op1=ALU.mult)
                else:
                    dve.drain()
                    for t in n:
                        last = nc.vector.tensor_scalar(dst[:, t, :], X[:, t, :], mv[:, t, 0:1], rstd[:, t:t + 1],
                                                       ALU.subtract, ALU.mult)
                    if done:
                        last.then_inc(sem(done), 1)

            def layer_norm(dst, eps):
                for step in range(4):
                    normalise(step, slice(0, NT), dst, eps)

            def outer_v(s):
                dve.wait_ge(sem("outer_in" + s), 16 * 8)
                dve.wait_ge(sem(s + "_v"), 1)
                for b in range(B):
                    last = nc.vector.tensor_tensor(vo[:, b, :], S_ps[1][:, b * P:(b + 1) * P], bv[s][:], ALU.add)
                last.then_inc(sem(s + "_v_sb"), 1)

            def token_softmax(s):
                outer_v(s)
                for b in range(B):
                    dve.wait_ge(sem(s + "_scores"), b + 1)
                    nc.vector.reduce_max(omax[0:M, b:b + 1], O_ps[b][0:M, :], AX)
                    dve.drain()
                    nc.vector.tensor_scalar(onmx[0:M, b:b + 1], omax[0:M, b:b + 1], -float(E) ** -0.5, None,
                                            ALU.mult).then_inc(sem(s + "_max"), 1)
                for b in range(B):
                    dve.wait_ge(sem(s + "_exp"), b + 1)
                    nc.vector.reciprocal(orec[0:M, b:b + 1], osum[0:M, b:b + 1])
                    dve.drain()
                    nc.vector.tensor_scalar(OP[0:M, b, :], OP[0:M, b, :], orec[0:M, b:b + 1], None, ALU.mult)\
                      .then_inc(sem(s + "_weights"), 1)
                for b in range(B):
                    dve.wait_ge(sem(s + "_pred"), b + 1)
                    rows = X[:, b * TB:(b + 1) * TB, :]
                    nc.vector.tensor_tensor(rows, tiles(W_ps[b][:]), rows, ALU.add)
                layer_norm(X, EPS_LATENT)
                dve.drain()
                for b in range(B):
                    rows = X[:, b * TB:(b + 1) * TB, :]
                    g = gam[s][:].unsqueeze(1).broadcast_to([P, TB, E])
                    nc.vector.tensor_tensor(rows, rows, g, ALU.mult)
                    dve.drain()
                    g = bet[s][:].unsqueeze(1).broadcast_to([P, TB, E])
                    nc.vector.tensor_tensor(rows, rows, g, ALU.add)\
                      .then_inc(sem("B_src" if s == "L0" else "out_ready"), 1)

            dve.wait_ge(sem("mask_in"), 32)
            nc.vector.tensor_scalar(self_bias[:], self_bias[:].bitcast(I32), 0, BIG, ALU.is_equal, ALU.mult)
            dve.wait_ge(sem("consts"), 1)
            nc.vector.tensor_scalar(cross_bias[:, :, 0:M], cmask_i[:], 0, BIG, ALU.is_equal, ALU.mult)
            dve.drain()
            nc.vector.tensor_reduce(bad[:, :, 0], self_bias[:, :, 0:KEYS], AX, ALU.min)
            nc.vector.tensor_reduce(bad[:, :, 1], self_bias[:, :, KEYS:T], AX, ALU.min)
            dve.drain()
            nc.vector.tensor_scalar(bad[:, :, 0], bad[:, :, 0], 0.0, None, ALU.is_equal)
            nc.vector.tensor_scalar(bad[:, :, 1], bad[:, :, 1], 0.0, None, ALU.is_gt)
            dve.drain()
            nc.vector.tensor_reduce(badp[:], bad[:].rearrange("p t a -> p (t a)"), AX, ALU.max)\
              .then_inc(sem("bad_rows"), 1)

            dve.wait_ge(sem("x_in"), 16)
            token_softmax("L0")
            outer_v("L1")
            for b in range(B):
                dve.wait_ge(sem("L1_scores"), b + 1)
                nc.vector.tensor_reduce(omax[:, b * TB:(b + 1) * TB], tiles(O_ps[b][:])[:, :, 0:M], AX, ALU.max)
                dve.drain()
                nc.vector.tensor_scalar(onmx[:, b * TB:(b + 1) * TB], omax[:, b * TB:(b + 1) * TB],
                                        -float(E) ** -0.5, None, ALU.mult).then_inc(sem("L1_max"), 1)
            for b in range(B):
                dve.wait_ge(sem("L1_exp"), b + 1)
                nc.vector.reciprocal(orec[:, b * TB:(b + 1) * TB], osum[:, b * TB:(b + 1) * TB])
                dve.drain()
                rows = XN[:, b * TB:(b + 1) * TB, 0:M]
                nc.vector.tensor_tensor(rows, rows, orec[:, b * TB:(b + 1) * TB].unsqueeze(2).broadcast_to([P, TB, M]),
                                        ALU.mult).then_inc(sem("L1_weights"), 1)
            nc.vector.tensor_tensor(X[:], X[:], bo1[:].unsqueeze(1).broadcast_to([P, NT, E]), ALU.add)
            dve.drain()
            for b in range(B):
                dve.wait_ge(sem("L1_out"), b + 1)
                rows = X[:, b * TB:(b + 1) * TB, :]
                nc.vector.tensor_tensor(rows, tiles(W_ps[b][:]), rows, ALU.add)
            dve.drain().then_inc(sem("L1_done"), 1)
            dve.wait_ge(sem("bad_sum"), 1)
            nc.vector.tensor_scalar(flag_f[:], O_ps[0][0:1, 0:1], 1.0, None, ALU.min)
            dve.drain()
            if force_all:
                nc.vector.tensor_scalar(flag[:], flag_f[:], 0.0, 1.0, ALU.mult, ALU.add).then_inc(sem("flag"), 1)
            else:
                nc.vector.tensor_copy(flag[:], flag_f[:]).then_inc(sem("flag"), 1)

            def prepare(b, step, bias):
                ts = slice(b * TB, (b + 1) * TB)
                if step < 4:
                    normalise(step, ts, XN, EPS_DEC, "xn_ready")
                else:
                    dve.drain()
                    nc.vector.tensor_tensor(X[:, ts, :], X[:, ts, :], bias[:].unsqueeze(1).broadcast_to([P, TB, E]),
                                            ALU.add)

            def work(ring, event, l, N):
                what, i = event
                if (ring.name, event) not in vector_empties:
                    return
                w = W_ps[ring.bank(event)]
                dve.wait_ge(sem(ring.full(event)), ring.value(event, l))
                if what == "n":
                    last = nc.vector.tensor_copy(N[:, i * TB:(i + 1) * TB, :], tiles(w[:]))
                elif what == "V":
                    last = nc.vector.tensor_copy(V[:, i % 2, :, :], tiles(w[:]))
                else:
                    rows = X[:, i * TB:(i + 1) * TB, :]
                    last = nc.vector.tensor_tensor(rows, tiles(w[:]), rows, ALU.add)
                last.then_inc(sem(ring.free(event)), 1)

            def attention(st, l, bias):
                C, ring = st.chunks, st.ring

                def masked(n):
                    g, qt, b, _ = st.where(n)
                    s = n % 2
                    w = T if st.wide else P
                    for t in range(T // w):
                        cols = slice(t * w, (t + 1) * w)
                        row_bias = cross_bias[:, b, :] if st.cross else self_bias[:, b * TB + qt, st.key_base:T]
                        last = nc.vector.tensor_tensor_reduce(out=Sm[:, s, cols], in0=S_ps[s][:, cols], in1=row_bias,
                                                              scale=1.0, scalar=3.4e38, op0=ALU.add, op1=ALU.min,
                                                              accum_out=mn[:, s, t:t + 1])
                    last.then_inc(sem(f"{st.name}_masked"), 1)

                def reciprocals(n):
                    k = 1 if st.wide else TB
                    if n + 2 < C:
                        dve.wait_ge(sem(f"{st.name}_scores"), l * C + n + 3)
                    dve.wait_ge(sem(f"{st.name}_exp"), l * C + n + 1)
                    nc.vector.reciprocal(rsum[:, n % 2, 0:k], sums[:, n % 2, 0:k]).then_inc(sem(f"{st.name}_rsum"), 1)

                def weights(n):
                    s = n % 2
                    dve.wait_ge(sem(f"{st.name}_rsum"), l * C + n + 1)
                    if st.wide:
                        last = nc.vector.tensor_scalar(Pb[:, s, :], Pb[:, s, :], rsum[:, s, 0:1], None, ALU.mult)
                    else:
                        last = nc.vector.tensor_tensor(tiles(Pb[:, s, :]), tiles(Pb[:, s, :]),
                                                       rsum[:, s, :].unsqueeze(2).broadcast_to([P, TB, P]), ALU.mult)
                    last.then_inc(sem(f"{st.name}_weights"), 1)

                for n in range(2):
                    dve.wait_ge(sem(f"{st.name}_scores"), l * C + n + 1)
                    nc.vector.memset(carrier[:, n:n + 1], 0.0)
                    masked(n)
                for n in range(C + TB + 1):
                    if n < C:
                        reciprocals(n)
                    if n + 2 < C:
                        masked(n + 2)
                    if n < C:
                        weights(n)
                    if n < C + TB:
                        for event in st.plan[n]:
                            work(ring, event, l, Nc)
                        for b, step in st.norm[n]:
                            prepare(b, step, bias(b))

            dve.wait_ge(sem("pads_zero"), 1)
            dve.wait_ge(sem("flag"), 1)
            general = dve.value_load(flag[0:1, 0:1], min_val=0, max_val=1)
            with dve.Fori(0, L) as l:
                for step in range(4):
                    prepare(0, step, sob)
                dve.wait_ge(sem("self_w"), SELF_W * l + SELF_W)
                dve.wait_ge(sem("cross_w"), SELF_W * l + SELF_W)
                nc.vector.memset(carrier[:, 2:3], 0.0)
                prepare(0, 4, sob)
                with dve.If(general > 0):
                    attention(SELF_ALL, l, lambda b: cob if b == 0 else sob)
                with dve.Else():
                    attention(SELF_LAST, l, lambda b: cob if b == 0 else sob)
                dve.wait_ge(sem("ff_w"), 96 * l + 96)
                nc.vector.memset(carrier[:, 3:4], 0.0)
                attention(CROSS, l, lambda b: b2 if b == 0 else cob)
                work(FFN, ("fin", 1), l, None)
                for step in range(5):
                    prepare(1, step, b2)
                dve.drain()
                for b in range(B):
                    dve.wait_ge(sem("ff_out"), l * B + b + 1)
                    rows = X[:, b * TB:(b + 1) * TB, :]
                    last = nc.vector.tensor_tensor(rows, tiles(T_ps[b][:]), rows, ALU.add)
                last.then_inc(sem("ff_done"), 1)
            dve.drain().then_inc(sem("C_src"), 2)
            token_softmax("L3")


_OUT_SHAPE = (2, 512, 128)


def kernel(**inputs):
    import numpy as _np
    import concourse.bacc as _bacc
    from concourse import mybir as _mybir
    from concourse.bass_utils import run_bass_kernel_spmd as _run

    nc = _bacc.Bacc("TRN2", target_bir_lowering=False, num_devices=1)
    arrays, args = {}, {}
    for name, value in inputs.items():
        v = _np.ascontiguousarray(value)
        arrays[f"in_{name}"] = v
        args[name] = nc.dram_tensor(f"in_{name}", v.shape, _mybir.dt.from_np(v.dtype), kind="ExternalInput").ap()
    out = nc.dram_tensor("out_x", _OUT_SHAPE, _mybir.dt.float32, kind="ExternalOutput").ap()
    build(nc, args, out)
    r = _run(nc, [arrays], core_ids=[0])
    return r.results[0]["out_x"]
```

```python
from contextlib import ExitStack

import concourse.bass as bass
from concourse import mybir

F32 = mybir.dt.float32
I32 = mybir.dt.int32
ALU = mybir.AluOpType
ACT = mybir.ActivationFunctionType
AX = mybir.AxisListType.X

B, T, E = 2, 512, 128
M, CD = 77, 64
L, H, D, FF = 6, 16, 64, 512
P = 128
NT = B * T // P
TB = T // P
NPAIR = H * D // P
NF = FF // P
KEYS = T - P
BIG = 1.0e30
EPS_LATENT, EPS_DEC = 1e-6, 1e-5
RSQRT_SEED = 0x5F3759DF
STEPS = 5
SLOTS = 5
BANKS = 3
TAIL = (0, 1)
AHEAD = 3
GM = 96
CBLK = 3
CW = -(-TB * M // CBLK)
CSTART = [j * CW for j in range(CBLK)] + [TB * M]
assert all(j * M <= CSTART[j] < (j + 1) * M < CSTART[j + 1] <= (j + 2) * M for j in range(CBLK))


class Ring:

    def __init__(self, name, order):
        self.name = name
        self.index = {e: i for i, e in enumerate(order)}
        self.total = [len(range(k, len(order), BANKS)) for k in range(BANKS)]
        assert len(self.index) == len(order)

    def bank(self, event):
        return self.index[event] % BANKS

    def count(self, event):
        return self.index[event] // BANKS + 1

    def full(self, event):
        return f"{self.name}_work_full{self.bank(event)}"

    def free(self, event):
        return f"{self.name}_work_free{self.bank(event)}"

    def value(self, event, l):
        return l * self.total[self.bank(event)] + self.count(event)


FOLD = [(k, i) for k in ("tq", "tk", "tv") for i in (0, 1)] + [(k, i) for k in ("m", "n") for i in range(4)]


class Group:

    def __init__(self, cross, wide, b, index, of):
        self.cross, self.wide, self.b, self.index = cross, wide, b, index
        self.heads = 1 if wide else TB
        self.keys = T if wide else M if cross else P
        self.columns = self.heads * self.keys
        self.key_base = 0 if wide else KEYS
        self.starts = CSTART if cross else [k * P for k in range(TB + 1)]
        self.blocks = len(self.starts) - 1
        self.rows = self.starts[1]
        self.first, self.last = index == 0, index == of - 1
        self.section = 2 * cross + b


class Stream:

    def __init__(self, name, wide):
        self.name = name
        self.groups = [Group(cross, w, b, i, of) for cross, w, of in ((0, wide, H if wide else H // TB), (1, False, H // TB))
                       for b in range(B) for i in range(of)]
        self.chunks = TB * len(self.groups)
        self.begin = [next(g for g, x in enumerate(self.groups) if x.section == k) for k in range(2 * B)]
        self.first = [("G", 0), ("G", 1)]
        self.plan = [[] for _ in range(self.chunks + TB)]
        self.norm = [[] for _ in range(self.chunks + TB + 2)]
        self.normalise(0, 1, None)
        for k in range(1, 2 * B):
            self.normalise(TB * self.begin[k] + TB, k + 1, k - 1)
        for g in range(len(self.groups)):
            if g > 1:
                self.plan[max(0, TB * g - SLOTS - 4)].append(("G", g))
            self.plan[TB * g].append(("V", g))
        for i, e in enumerate(FOLD):
            self.plan[TB - 1 + i].append(e)
        self.ring = Ring(name, self.first + [e for step in self.plan for e in step])
        self.attended = [sum(x.blocks - x.last for x in self.groups[:g]) for g in range(len(self.groups) + 1)]

    def normalise(self, at, k, fin):
        if fin is not None:
            self.plan[at].append(("fin", fin))
            at += 1
        for step in range(STEPS + 1):
            self.norm[at + 1 + step].append((k, step))
        self.plan[at + STEPS].insert(0, ("xn", k))


STREAM_ALL = Stream("all_keys", True)
STREAM_LAST = Stream("last_keys", False)
TOP = Ring("top", FOLD[:-2] + [("xn", 0)] + FOLD[-2:])
FFN = Ring("ffn", [("fin", 3), ("xn", 5)])


vector_empties = {(s.ring.name, e) for s in (STREAM_ALL, STREAM_LAST) for e in s.ring.index
                  if e[0] in ("V", "fin", "n")} | {("ffn", ("fin", 3))}
SELF_W, CROSS_W = 16 * 5, 16 * 6


def build(nc, a, out):
    with ExitStack() as ctx:
        def sb(name, shape, dt=F32):
            return ctx.enter_context(nc.sbuf_tensor(name, shape, dt))

        sems = {}

        def sem(name):
            if name not in sems:
                sems[name] = ctx.enter_context(nc.semaphore(name))
            return sems[name]

        ident = sb("ident", [P, P])
        ones = sb("ones", [P, 1])
        X = sb("X", [P, NT, E])
        XN = sb("XN", [P, NT, E])
        XT = sb("XT", [P, B * T])
        ctx_in = sb("ctx_in", [P, B, 2, CD])
        ctxT = sb("ctxT", [P, B, P])
        ctxV = sb("ctxV", [P, B, CBLK, CW])
        self_bias = sb("self_bias", [P, NT, T])
        cmask_i = sb("cmask_i", [P, B, M], I32)
        cross_bias = sb("cross_bias", [P, B, M])
        stats = sb("stats", [P, NT, 6])
        mv = sb("mv", [P, NT, 2])
        veps = sb("veps", [P, NT])
        rstd = sb("rstd", [P, NT])
        newton = sb("newton", [P, NT])
        oT = sb("oT", [P, B, T])
        wqT = sb("wqT", [P, NPAIR, 2, E])
        wkT = sb("wkT", [P, NPAIR, E])
        wvT = sb("wvT", [P, NPAIR, E])
        Ms, Mc = sb("Ms", [P, H, E]), sb("Mc", [P, H, E])
        Ns = sb("Ns", [P, H, E])
        Nc = sb("Nc", [P, H // TB, CBLK, E])
        G = sb("G", [P, 2, T])
        qT = G[:].rearrange("p s k -> p (s k)")
        V = sb("V", [P, 2, TB, E])
        Sm = sb("Sm", [P, SLOTS, T])
        Pb = sb("Pb", [P, SLOTS, T])
        PT = sb("PT", [P, 2, TB, T])
        mn = sb("mn", [P, SLOTS, TB])
        sums = sb("sums", [P, SLOTS, TB])
        rsum = sb("rsum", [P, SLOTS, TB])
        hT = sb("hT", [P, B, NF, T])
        saq, sakv = sb("saq", [P, H * D]), sb("sakv", [P, 2 * H * D])
        saow = sb("saow", [P, NPAIR, 2, E])
        caq, cakv = sb("caq", [P, H * D]), sb("cakv", [P, 2 * H * D])
        caow = sb("caow", [P, NPAIR, 2, E])
        w1, w2 = sb("w1", [P, FF]), sb("w2", [P, NF, E])
        sob, cob, b2 = sb("sob", [P, E]), sb("cob", [P, E]), sb("b2", [P, E])
        b1 = sb("b1", [P, NF])
        pre_g, pre_b = sb("pre_g", [P, 1]), sb("pre_b", [P, 1])
        norm_g, norm_b = sb("norm_g", [P, 1]), sb("norm_b", [P, 1])
        OUTER = ["L0", "L1", "L3"]
        wq = {s: sb(f"{s}wq", [P, P]) for s in OUTER}
        wk = {s: sb(f"{s}wk", [CD, P]) for s in OUTER}
        wv = {s: sb(f"{s}wv", [CD, P]) for s in OUTER}
        bq = {s: sb(f"{s}bq", [P, 1]) for s in OUTER}
        bk = {s: sb(f"{s}bk", [P, 1]) for s in OUTER}
        bv = {s: sb(f"{s}bv", [P, P]) for s in OUTER}
        gam = {s: sb(f"{s}gam", [P, P]) for s in ("L0", "L3")}
        bet = {s: sb(f"{s}bet", [P, P]) for s in ("L0", "L3")}
        wo1, bo1 = sb("wo1", [P, P]), sb("bo1", [P, P])
        kT = sb("kT", [P, B, P])
        vo = sb("vo", [P, B, P])
        omax = sb("omax", [P, NT])
        onmx = sb("onmx", [P, NT])
        osum = sb("osum", [P, NT])
        orec = sb("orec", [P, NT])
        OP = sb("OP", [P, B, T])
        carrier = sb("carrier", [P, SLOTS + 2])
        bad = sb("bad", [P, NT, 2])
        badp = sb("badp", [P, 1])
        flag_f = sb("flag_f", [1, 1])
        flag = sb("flag", [1, 1], I32)

        def bank(name):
            return ctx.enter_context(nc.psum_tensor(name, [P, T], F32))

        S_ps = [bank("S0"), bank("S1")]
        T_ps = [bank("T0"), bank("T1")]
        sum_ps = bank("sum")
        W_ps = [bank("W0"), bank("W1"), bank("W2")]
        O_ps = [sum_ps, W_ps[2]]

        def tiles(ap):
            return ap.rearrange("p (t e) -> p t e", e=P)

        def row(v):
            return v.rearrange("(a n) -> a n", a=1).broadcast_to([P, v.shape[0]])

        def by_key(ap, group):
            return ap[:, 0:group.columns].rearrange("p (h k) -> p h k", k=group.keys)

        def col(v):
            return v.rearrange("(p a) -> p a", a=1)

        block = ctx.enter_context(nc.Block())

        @block.sync
        def _(sp):
            sp.dma_start(X[:], a["x"].rearrange("b (t p) e -> p (b t) e", p=P)).then_inc(sem("x_in"), 16)
            for b in range(B):
                for twice in range(2):
                    sp.dma_start(ctx_in[0:M, b, twice, :], a["ctx_512"][b]).then_inc(sem("ctx_in"), 16)
            for s in OUTER:
                w = f"{s}_xattn_"
                for dst, src in ((wq[s][:], a[w + "Wq"]), (wk[s][:], a[w + "Wk"]), (wv[s][:], a[w + "Wv"]),
                                 (bq[s][:], col(a[w + "bq"])), (bk[s][:], col(a[w + "bk"])),
                                 (bv[s][:], row(a[w + "bv"]))):
                    sp.dma_start(dst, src).then_inc(sem("outer_in" + s), 16)
                if s == "L1":
                    sp.dma_start(wo1[:], a[w + "Wo"]).then_inc(sem("outer_inL1"), 16)
                    sp.dma_start(bo1[:], row(a[w + "bo"])).then_inc(sem("outer_inL1"), 16)
                else:
                    sp.dma_start(gam[s][:], row(a[w + "gamma"])).then_inc(sem("outer_in" + s), 16)
                    sp.dma_start(bet[s][:], row(a[w + "beta"])).then_inc(sem("outer_in" + s), 16)
                if s == "L0":
                    sp.dma_start(self_bias[:].bitcast(I32), a["mask_BxSxS_ik0"].rearrange("b (t p) k -> p (b t) k", p=P))\
                      .then_inc(sem("mask_in"), 16)
                    sp.dma_start(cmask_i[:], a["mask_Bx1xS2_if1"].rearrange("b a m -> a b m").broadcast_to([P, B, M]))\
                      .then_inc(sem("mask_in"), 16)
                    sp.dma_start(norm_g[:], col(a["L2_xattn_norm_g"])).then_inc(sem("norm_in"), 16)
                    sp.dma_start(norm_b[:], col(a["L2_xattn_norm_b"])).then_inc(sem("norm_in"), 16)

            def layer(name, l):
                v = a["L2_xattn_" + name]
                v = v[bass.ds(l, 1)]
                return v.rearrange("a p n -> p (a n)") if len(v.shape) == 3 else v

            def heads(name, l):
                return a["L2_xattn_" + name][bass.ds(l, 1)].rearrange("a (g p) n -> p (a g) n", p=P)

            def load_self(l):
                for dst, src in ((saq[:], layer("sa_q", l)), (sakv[:], layer("sa_kv", l)),
                                 (saow[0:D, :, 0, :], heads("sa_ow", l)[0:D]), (saow[D:P, :, 1, :], heads("sa_ow", l)[D:P]),
                                 (sob[:], layer("sa_ob", l).broadcast_to([P, E]))):
                    sp.dma_start(dst, src).then_inc(sem("self_w"), 16)

            def load_cross(l):
                for dst, src in ((caq[:], layer("ca_q", l)), (cakv[0:CD, :], layer("ca_kv", l)),
                                 (cakv[CD:P, :], layer("ca_kv", l)),
                                 (caow[0:D, :, 0, :], heads("ca_ow", l)[0:D]), (caow[D:P, :, 1, :], heads("ca_ow", l)[D:P]),
                                 (cob[:], layer("ca_ob", l).broadcast_to([P, E]))):
                    sp.dma_start(dst, src).then_inc(sem("cross_w"), 16)

            def load_ff(l):
                for dst, src in ((w1[:], layer("ff_w1", l)),
                                 (w2[:], a["L2_xattn_ff_w2"][bass.ds(l, 1)].rearrange("a (g p) n -> p (a g) n", p=P)),
                                 (b2[:], layer("ff_b2", l).broadcast_to([P, E])),
                                 (b1[:], layer("ff_b1", l).rearrange("a (g p) -> p (a g)", p=P)),
                                 (pre_g[:], layer("pre_g", l).rearrange("a p -> p a")),
                                 (pre_b[:], layer("pre_b", l).rearrange("a p -> p a"))):
                    sp.dma_start(dst, src, allow_slow_non_contiguous=True).then_inc(sem("ff_w"), 16)

            sp.wait_ge(sem("pads_zero"), 1)
            load_self(0)
            load_cross(0)
            load_ff(0)
            with sp.Fori(0, L - 1) as l:
                sp.wait_ge(sem("out_sum"), 4 * l + 1)
                load_self(l + 1)
                sp.wait_ge(sem("out_sum"), 4 * l + 3)
                load_cross(l + 1)
                sp.wait_ge(sem("ff_done"), l + 1)
                load_ff(l + 1)
            for b in range(B):
                sp.wait_ge(sem("out_ready"), b + 1)
                sp.dma_start(out[b].rearrange("(t p) e -> p t e", p=P), X[:, b * TB:(b + 1) * TB, :])\
                  .then_inc(sem("out_done"), 16)
            sp.wait_ge(sem("out_done"), 32)

        @block.gpsimd
        def _(gp):
            nc.gpsimd.memset(saow[D:P, :, 0, :], 0.0).then_inc(sem("gp_pad"), 1)
            nc.gpsimd.memset(saow[0:D, :, 1, :], 0.0).then_inc(sem("gp_pad"), 1)
            nc.gpsimd.memset(caow[D:P, :, 0, :], 0.0).then_inc(sem("gp_pad"), 1)
            nc.gpsimd.memset(caow[0:D, :, 1, :], 0.0).then_inc(sem("gp_pad"), 1)
            nc.gpsimd.memset(wqT[D:P, :, 0, :], 0.0).then_inc(sem("gp_pad"), 1)
            nc.gpsimd.memset(wqT[0:D, :, 1, :], 0.0).then_inc(sem("gp_pad"), 1)
            gp.wait_ge(sem("gp_pad"), 6)
            nc.gpsimd.memset(ident[:], 0.0).then_inc(sem("gp_zero"), 1)
            nc.gpsimd.memset(ones[:], 1.0).then_inc(sem("gp_zero"), 1)
            nc.gpsimd.memset(ctxT[:], 0.0).then_inc(sem("gp_zero"), 1)
            nc.gpsimd.memset(ctxV[:], 0.0).then_inc(sem("gp_zero"), 1)
            gp.wait_ge(sem("gp_zero"), 4)
            nc.gpsimd.affine_select(out=ident[:], in_=ident[:], compare_op=ALU.not_equal, fill=1.0, base=0,
                                    pattern=[[-1, P]], channel_multiplier=1).then_inc(sem("consts"), 1)
            gp.wait_ge(sem("consts"), 1)
            nc.gpsimd.memset(carrier[:], 0.0).then_inc(sem("pads_zero"), 1)

            def attention(st, l):
                for n in range(st.chunks):
                    s, group = n % SLOTS, st.groups[n // TB]
                    gp.wait_ge(sem(f"{st.name}_rsum"), l * st.chunks + n + 1)
                    if group.wide:
                        rows, r = tiles(Pb[:, s, :]), rsum[:, s, 0:1].unsqueeze(2).broadcast_to([P, TB, P])
                    else:
                        rows, r = by_key(Pb[:, s, :], group), rsum[:, s, :].unsqueeze(2).broadcast_to([P, TB, group.keys])
                    nc.gpsimd.tensor_tensor(rows, rows, r, ALU.mult).then_inc(sem(f"{st.name}_weights"), 1)

            gp.wait_ge(sem("flag"), 1)
            general = gp.value_load(flag[0:1, 0:1], min_val=0, max_val=1)
            with gp.Fori(0, L) as l:
                with gp.If(general > 0):
                    attention(STREAM_ALL, l)
                with gp.Else():
                    attention(STREAM_LAST, l)

        @block.tensor
        def _(pe):
            def transposes(src, bank, n, name):
                for t in range(TB):
                    last = nc.tensor.transpose(bank[:, t * P:(t + 1) * P], src[:, n * TB + t, :], ident[:])
                last.then_inc(sem(name), 1)

            def to_features(src, name):
                for b in range(B):
                    pe.wait_ge(sem(name + "_src"), b + 1)
                    transposes(src, T_ps[b], b, name + "_turned")

            def outer_projections(s, nb):
                pe.wait_ge(sem("outer_in" + s), 16 * 8)
                for b in range(B):
                    pe.wait_ge(sem(nb + "_xt"), b + 1)
                    nc.tensor.matmul(W_ps[b][:], wq[s][:], XT[:, b * T:(b + 1) * T], start=True, stop=True)\
                      .then_inc(sem(s + "_q"), 1)
                nc.tensor.matmul(S_ps[0][:, 0:B * P], wk[s][:], ctxT[0:CD].rearrange("c b m -> c (b m)"),
                                 start=True, stop=True).then_inc(sem(s + "_k"), 1)
                for b in range(B):
                    last = nc.tensor.matmul(S_ps[1][:, b * P:(b + 1) * P], ctxT[0:CD, b, :], wv[s][:],
                                            start=True, stop=True)
                last.then_inc(sem(s + "_v"), 1)

            def token_softmax(s, nb):
                outer_projections(s, nb)
                for b in range(B):
                    pe.wait_ge(sem(s + "_qk_sb"), 3)
                    nc.tensor.matmul(O_ps[b][0:M, :], kT[:, b, 0:M], qT[:, b * T:(b + 1) * T],
                                     start=True, stop=True).then_inc(sem(s + "_scores"), 1)
                for b in range(B):
                    pe.wait_ge(sem(s + "_weights"), b + 1)
                    pe.wait_ge(sem(s + "_v_sb"), 1)
                    for t in range(TB):
                        last = nc.tensor.matmul(W_ps[b][:, t * P:(t + 1) * P], OP[0:M, b, t * P:(t + 1) * P],
                                                vo[0:M, b, :], start=True, stop=True)
                    last.then_inc(sem(s + "_pred"), 1)

            pe.wait_ge(sem("consts"), 1)
            pe.wait_ge(sem("ctx_in"), 16 * 2 * B)
            for b in range(B):
                last = nc.tensor.transpose(S_ps[0][:, b * P:b * P + M], ctx_in[0:M, b, :, :].rearrange("m a c -> m (a c)"),
                                           ident[0:M, 0:M])
            last.then_inc(sem("ctx_turned"), 1)
            pe.wait_ge(sem("x_in"), 16)
            for b in range(B):
                transposes(X, T_ps[b], b, "A_turned")
            pe.wait_ge(sem("ctx_sb"), 2)
            token_softmax("L0", "A")
            to_features(X, "B")
            outer_projections("L1", "B")
            pe.wait_ge(sem("L1_qk_sb"), 3)
            for b in range(B):
                for t in range(TB):
                    last = nc.tensor.matmul(O_ps[b][:, t * P:t * P + M],
                                            qT[:, (b * TB + t) * P:(b * TB + t + 1) * P], kT[:, b, 0:M],
                                            start=True, stop=True)
                last.then_inc(sem("L1_scores"), 1)
            for b in range(B):
                pe.wait_ge(sem("L1_weights"), b + 1)
                for t in range(TB):
                    last = nc.tensor.transpose(T_ps[b][0:M, t * P:(t + 1) * P], XN[:, b * TB + t, 0:M], ident[:])
                last.then_inc(sem("L1_turned"), 1)
            pe.wait_ge(sem("L1_v_sb"), 1)
            for b in range(B):
                pe.wait_ge(sem("L1_wT"), b + 1)
                nc.tensor.matmul(S_ps[b][:], vo[0:M, b, :], OP[0:M, b, :], start=True, stop=True)\
                  .then_inc(sem("L1_att"), 1)
            for b in range(B):
                pe.wait_ge(sem("L1_att_sb"), b + 1)
                for t in range(TB):
                    last = nc.tensor.matmul(W_ps[b][:, t * P:(t + 1) * P], oT[:, b, t * P:(t + 1) * P], wo1[:],
                                            start=True, stop=True)
                last.then_inc(sem("L1_out"), 1)
            pe.wait_ge(sem("bad_rows"), 1)
            pe.wait_ge(sem("L1_done"), 1)
            nc.tensor.matmul(O_ps[0][0:1, 0:1], badp[:], ones[:], start=True, stop=True).then_inc(sem("bad_sum"), 1)

            def read(ring, events, l, to_fill=None):
                need = [0] * BANKS
                for e in events:
                    need[ring.bank(e)] = max(need[ring.bank(e)], ring.count(e))
                if to_fill is not None:
                    k = ring.bank(to_fill)
                    need[k] = max(need[k], ring.count(to_fill) - 1)
                for k in range(BANKS):
                    if need[k]:
                        pe.wait_ge(sem(f"{ring.name}_work_free{k}"), l * ring.total[k] + need[k])

            def pair_tiles(w, i):
                return [(j, w[:, (i * TB + j) * P:(i * TB + j + 1) * P]) for j in range(TB)]

            def work(ring, event, l, q, kv, ow, st=None):
                what, i = event
                w = W_ps[ring.bank(event)]
                before = []
                if event == ("m", 0):
                    before = [(k, j) for k in ("tq", "tk") for j in range(2)]
                elif event == ("n", 0):
                    before = [("tv", 0), ("tv", 1)]
                elif what in ("G", "V"):
                    group = st.groups[i]
                    b, g = group.b, group.index
                    M, N = (Mc, Nc) if group.cross else (Ms, Ns)
                    if what == "G" and group.first and group.section == 1:
                        before = [("xn", 1)]
                    elif group.first and group.section == 2:
                        before = [("m" if what == "G" else "n", k) for k in range(TB)]
                if st and ring.count(event) == 1:
                    k = ring.bank(event)
                    pe.wait_ge(sem(f"top_work_free{k}"), l * TOP.total[k] + TOP.total[k])
                read(ring, before, l, to_fill=event)
                if what in ("tq", "tk", "tv"):
                    src = {"tq": q, "tk": kv, "tv": kv[:, H * D:]}[what]
                    for j, cols in pair_tiles(src, i):
                        last = nc.tensor.transpose(w[:, j * P:(j + 1) * P], cols, ident[:])
                elif what in ("m", "n"):
                    for j in range(2):
                        p = 2 * i + j
                        lhs, rhs = (wkT, wqT) if what == "m" else (wvT, ow)
                        last = nc.tensor.matmul(w[:, j * 2 * E:(j + 1) * 2 * E], lhs[:, p, :],
                                                rhs[:, p, :, :].rearrange("p h e -> p (h e)"), start=True, stop=True)
                elif what == "G":
                    if group.wide:
                        last = nc.tensor.matmul(w[:], M[:, g, :], XT[:, b * T:(b + 1) * T], start=True, stop=True)
                    else:
                        keys = ctxT[:, b, 0:GM] if group.cross else XT[:, b * T + KEYS:(b + 1) * T]
                        for j in range(TB):
                            last = nc.tensor.matmul(w[:, j * P:j * P + keys.shape[1]], M[:, g * TB + j, :], keys,
                                                    start=True, stop=True)
                elif what == "V":
                    if group.wide:
                        for j in range(TB):
                            last = nc.tensor.matmul(w[:, j * P:(j + 1) * P],
                                                    XT[:, b * T + j * P:b * T + (j + 1) * P], N[:, g, :],
                                                    start=True, stop=True)
                    elif group.cross:
                        for j in range(CBLK):
                            last = nc.tensor.matmul(w[0:CW, j * P:(j + 1) * P], ctxV[:, b, j, :], N[:, g, j, :],
                                                    start=True, stop=True)
                    else:
                        keys = XT[:, b * T + KEYS:(b + 1) * T]
                        last = nc.tensor.matmul(w[:], keys, N[:, g * TB:(g + 1) * TB, :].rearrange("p h e -> p (h e)"),
                                                start=True, stop=True)
                elif what == "fin":
                    pe.wait_ge(sem("oT_sb"), l * 2 * B + i + 1)
                    for t in range(TB):
                        last = nc.tensor.transpose(w[:, t * P:(t + 1) * P], oT[:, i % B, t * P:(t + 1) * P], ident[:])
                else:
                    pe.wait_ge(sem("xn_ready"), l * 3 * B + i + 1)
                    for t in range(TB):
                        last = nc.tensor.transpose(w[:, t * P:(t + 1) * P], XN[:, i % B * TB + t, :], ident[:])
                last.then_inc(sem(ring.full(event)), 1)

            def all_read(ring, l):
                for k in range(BANKS):
                    if ring.total[k]:
                        pe.wait_ge(sem(f"{ring.name}_work_free{k}"), l * ring.total[k] + ring.total[k])

            def hidden(l, b, f):
                i = b * NF + f
                if i >= 2:
                    pe.wait_ge(sem("hidden_sb"), l * B * NF + i - 1)
                nc.tensor.matmul(S_ps[i % 2][:], w1[:, f * P:(f + 1) * P], XT[:, b * T:(b + 1) * T],
                                 start=True, stop=True).then_inc(sem("hidden"), 1)

            def attention(st, l):
                C, ring = st.chunks, st.ring

                def do(event):
                    work(ring, event, l, caq, cakv, caow, st)

                def scores(n):
                    g, qt = divmod(n, TB)
                    group = st.groups[g]
                    b, k = group.b, group.section
                    if qt == 0:
                        read(ring, [("G", g)] + [("xn", k)] * (group.first and k > 0), l)
                    if n >= len(S_ps):
                        pe.wait_ge(sem(f"{st.name}_masked"), l * C + n - len(S_ps) + 1)
                    nc.tensor.matmul(S_ps[n % len(S_ps)][:, 0:group.columns], XT[:, (b * TB + qt) * P:(b * TB + qt + 1) * P],
                                     G[:, g % 2, 0:group.columns], start=True, stop=True).then_inc(sem(f"{st.name}_scores"), 1)

                def turn(n):
                    pe.wait_ge(sem(f"{st.name}_weights"), l * C + n + 1)
                    if n >= 2:
                        pe.wait_ge(sem(f"{st.name}_turned_sb"), l * C + n - 1)
                    group = st.groups[n // TB]
                    for t in range(group.blocks):
                        k0, k1 = group.starts[t:t + 2]
                        last = nc.tensor.transpose(T_ps[n % 2][0:k1 - k0, t * P:(t + 1) * P],
                                                   Pb[:, n % SLOTS, k0:k1], ident[:])
                    last.then_inc(sem(f"{st.name}_turned"), 1)

                def attend(n):
                    g = n // TB - 1
                    group = st.groups[g]
                    blk = n % TB - (TB - group.blocks)
                    if blk < 0:
                        return
                    k = group.starts[blk + 1] - group.starts[blk]
                    if blk == 0:
                        pe.wait_ge(sem(f"{st.name}_turned_sb"), l * C + (g + 1) * TB)
                        read(ring, [("V", g)], l)
                        if group.first and group.section > 0:
                            pe.wait_ge(sem("oT_sb"), l * 2 * B + group.section)
                    done = group.last and blk == group.blocks - 1
                    nc.tensor.matmul(sum_ps[:], V[0:k, g % 2, blk, :], PT[0:k, g % 2, blk, :],
                                     start=(group.first and blk == 0), stop=done)\
                      .then_inc(sem("out_sum" if done else f"{st.name}_attended"), 1)

                for event in st.first:
                    do(event)
                for n in range(SLOTS):
                    scores(n)
                for n in range(C + TB):
                    if n + SLOTS < C:
                        scores(n + SLOTS)
                    if n >= TB:
                        attend(n)
                    f = n - (C - TB)
                    if f in TAIL:
                        if f == 0:
                            pe.wait_ge(sem("ff_w"), 96 * l + 96)
                            read(ring, [("xn", 2 * B)], l)
                        pe.wait_ge(sem(f"{st.name}_masked"), l * C + C - 1 + f)
                        hidden(l, 0, f)
                    for event in st.plan[n]:
                        if event[0] == "xn":
                            do(event)
                    if n < C:
                        turn(n)
                    for event in st.plan[n]:
                        if event[0] != "xn":
                            do(event)
                all_read(ring, l)

            pe.wait_ge(sem("pads_zero"), 1)
            pe.wait_ge(sem("flag"), 1)
            general = pe.value_load(flag[0:1, 0:1], min_val=0, max_val=1)
            with pe.Fori(0, L) as l:
                pe.wait_ge(sem("self_w"), SELF_W * l + SELF_W)
                for event in TOP.index:
                    work(TOP, event, l, saq, sakv, saow)
                read(TOP, [("m", k) for k in range(TB)] + [("xn", 0)], l)
                pe.wait_ge(sem("cross_w"), CROSS_W * l + CROSS_W)
                with pe.If(general > 0):
                    attention(STREAM_ALL, l)
                with pe.Else():
                    attention(STREAM_LAST, l)
                pe.wait_ge(sem("ff_w"), 96 * l + 96)

                def ff_out(b, tiles_of_batch):
                    pe.wait_ge(sem("hidden_sb"), l * B * NF + (b + 1) * NF)
                    for t in tiles_of_batch:
                        for f in range(NF):
                            last = nc.tensor.matmul(T_ps[b][:, t * P:(t + 1) * P], hT[:, b, f, t * P:(t + 1) * P],
                                                    w2[:, f, :], start=(f == 0), stop=(f == NF - 1))
                    if t == TB - 1:
                        last.then_inc(sem("ff_out"), 1)

                hidden(l, 0, 2)
                work(FFN, ("fin", 3), l, None, None, None)
                hidden(l, 0, 3)
                ff_out(0, range(TB - 1))
                work(FFN, ("xn", 5), l, None, None, None)
                ff_out(0, [TB - 1])
                read(FFN, [("xn", 5)], l)
                for f in range(NF):
                    hidden(l, 1, f)
                ff_out(1, range(TB))
            to_features(X, "C")
            token_softmax("L3", "C")

        @block.scalar
        def _(act):
            def features(name, bias=None):
                for b in range(B):
                    act.wait_ge(sem(name + "_turned"), b + 1)
                    nc.scalar.activation(XT[:, b * T:(b + 1) * T], T_ps[b][:], ACT.Copy).then_inc(sem(name + "_xt"), 1)

            def outer_evacuations(s):
                act.wait_ge(sem("outer_in" + s), 16 * 8)
                for b in range(B):
                    act.wait_ge(sem(s + "_q"), b + 1)
                    nc.scalar.activation(qT[:, b * T:(b + 1) * T], W_ps[b][:], ACT.Identity, bias=bq[s][:])\
                      .then_inc(sem(s + "_qk_sb"), 1)
                act.wait_ge(sem(s + "_k"), 1)
                nc.scalar.activation(kT[:].rearrange("p b m -> p (b m)"), S_ps[0][:, 0:B * P], ACT.Identity,
                                     bias=bk[s][:]).then_inc(sem(s + "_qk_sb"), 1)

            act.wait_ge(sem("ctx_turned"), 1)
            act.wait_ge(sem("consts"), 1)
            nc.scalar.activation(ctxT[0:CD, :, 0:M], S_ps[0][0:CD, 0:B * P].rearrange("c (b m) -> c b m", b=B)[:, :, 0:M],
                                 ACT.Copy).then_inc(sem("ctx_sb"), 1)

            def token_softmax(s):
                outer_evacuations(s)
                for b in range(B):
                    act.wait_ge(sem(s + "_max"), b + 1)
                    nc.scalar.activation(OP[0:M, b, :], O_ps[b][0:M, :], ACT.Exp, bias=onmx[0:M, b:b + 1],
                                         scale=float(E) ** -0.5, accum_out=osum[0:M, b:b + 1])\
                      .then_inc(sem(s + "_exp"), 1)

            features("A")
            token_softmax("L0")
            features("B")
            outer_evacuations("L1")
            for b in range(B):
                act.wait_ge(sem("L1_max"), b + 1)
                for t in range(TB):
                    i = b * TB + t
                    last = nc.scalar.activation(XN[:, i, 0:M], O_ps[b][:, t * P:t * P + M], ACT.Exp,
                                                bias=onmx[:, i:i + 1], scale=float(E) ** -0.5,
                                                accum_out=osum[:, i:i + 1])
                last.then_inc(sem("L1_exp"), 1)
            for b in range(B):
                act.wait_ge(sem("L1_turned"), b + 1)
                nc.scalar.activation(OP[0:M, b, :], T_ps[b][0:M, :], ACT.Copy).then_inc(sem("L1_wT"), 1)
            for b in range(B):
                act.wait_ge(sem("L1_att"), b + 1)
                nc.scalar.activation(oT[:, b, :], S_ps[b][:], ACT.Copy).then_inc(sem("L1_att_sb"), 1)

            def work(ring, event, l, M, N, st=None):
                what, i = event
                if (ring.name, event) in vector_empties:
                    return
                w = W_ps[ring.bank(event)]
                act.wait_ge(sem(ring.full(event)), ring.value(event, l))
                rows = slice(i * TB, (i + 1) * TB)
                if what == "tq":
                    for h, half in enumerate((slice(0, D), slice(D, P))):
                        last = nc.scalar.activation(wqT[half, rows, h, :], tiles(w[half, :]), ACT.Copy,
                                                    scale=-float(D) ** -0.5)
                elif what in ("tk", "tv"):
                    last = nc.scalar.activation((wkT if what == "tk" else wvT)[:, rows, :], tiles(w[:]), ACT.Copy)
                elif what in ("m", "n"):
                    last = nc.scalar.activation((M if what == "m" else N)[:, rows, :], tiles(w[:]), ACT.Copy)
                elif what == "G" and st.groups[i].cross:
                    group = st.groups[i]
                    last = nc.scalar.activation(by_key(G[:, i % 2, :], group), tiles(w[:])[:, :, 0:group.keys], ACT.Copy)
                elif what == "G":
                    last = nc.scalar.activation(G[:, i % 2, :], w[:], ACT.Copy)
                else:
                    g, bb = (pre_g, pre_b) if i >= 2 * B else (norm_g, norm_b)
                    if i == 2 * B:
                        act.wait_ge(sem("ff_w"), 96 * l + 96)
                    i %= B
                    last = nc.scalar.activation(XT[:, i * T:(i + 1) * T], w[:], ACT.Identity, bias=bb[:], scale=g[:])
                last.then_inc(sem(ring.free(event)), 1)

            def relu(l, b, f):
                i = b * NF + f
                act.wait_ge(sem("hidden"), l * B * NF + i + 1)
                nc.scalar.activation(hT[:, b, f, :], S_ps[i % 2][:], ACT.Relu, bias=b1[:, f:f + 1])\
                  .then_inc(sem("hidden_sb"), 1)

            def attention(st, l):
                C, ring = st.chunks, st.ring

                def exponentials(n):
                    act.wait_ge(sem(f"{st.name}_masked"), l * C + n + 1)
                    if n >= SLOTS:
                        act.wait_ge(sem(f"{st.name}_turned"), l * C + n - SLOTS + 1)
                    s = n % SLOTS
                    group = st.groups[n // TB]
                    w = group.keys
                    for t in range(group.heads):
                        last = nc.scalar.activation(Pb[:, s, t * w:(t + 1) * w], Sm[:, s, t * w:(t + 1) * w], ACT.Exp,
                                                    bias=mn[:, s, t:t + 1], scale=-1.0, accum_out=sums[:, s, t:t + 1])
                    last.then_inc(sem(f"{st.name}_exp"), 1)

                def evacuate_turned(n):
                    gr, qt = divmod(n, TB)
                    group = st.groups[gr]
                    act.wait_ge(sem(f"{st.name}_turned"), l * C + n + 1)
                    if gr >= 2 and qt == 0:
                        if st.groups[gr - 2].last:
                            act.wait_ge(sem("out_sum"), l * 2 * B + st.groups[gr - 2].section + 1)
                        act.wait_ge(sem(f"{st.name}_attended"), l * st.attended[-1] + st.attended[gr - 1])
                    nc.scalar.activation(PT[0:group.rows, gr % 2, 0:group.blocks, qt * P:(qt + 1) * P],
                                         tiles(T_ps[n % 2][0:group.rows, 0:group.blocks * P]), ACT.Copy)\
                      .then_inc(sem(f"{st.name}_turned_sb"), 1)

                for event in st.first:
                    work(ring, event, l, Mc, Nc, st)
                for n in range(AHEAD):
                    exponentials(n)
                for n in range(C + TB + 1):
                    if n + AHEAD < C:
                        exponentials(n + AHEAD)
                    for event in st.plan[n - 1] if n > 0 else []:
                        if event[0] != "xn":
                            work(ring, event, l, Mc, Nc, st)
                    for event in st.plan[n] if n < C + TB else []:
                        if event[0] == "xn":
                            work(ring, event, l, Mc, Nc, st)
                    if n < C:
                        evacuate_turned(n)
                    if n - 1 - (C - TB) in TAIL:
                        relu(l, 0, n - 1 - (C - TB))
                    g = n // TB - 1
                    if g in range(len(st.groups)) and st.groups[g].last and n % TB == TB - 1:
                        k = st.groups[g].section
                        act.wait_ge(sem("out_sum"), l * 2 * B + k + 1)
                        nc.scalar.activation(oT[:, k % B, :], sum_ps[:], ACT.Copy).then_inc(sem("oT_sb"), 1)

            act.wait_ge(sem("norm_in"), 32)
            act.wait_ge(sem("pads_zero"), 1)
            act.wait_ge(sem("flag"), 1)
            general = act.value_load(flag[0:1, 0:1], min_val=0, max_val=1)
            with act.Fori(0, L) as l:
                for event in TOP.index:
                    work(TOP, event, l, Ms, Ns)
                with act.If(general > 0):
                    attention(STREAM_ALL, l)
                with act.Else():
                    attention(STREAM_LAST, l)

                for f in range(len(TAIL), NF):
                    relu(l, 0, f)
                work(FFN, ("xn", 5), l, None, None)
                for f in range(NF):
                    relu(l, 1, f)
            features("C")
            token_softmax("L3")

        @block.vector
        def _(dve):
            def normalise(step, ts, dst, eps, done=None):
                v, r, w = veps[:, ts], rstd[:, ts], newton[:, ts]
                n = range(ts.start, ts.stop)
                if step == 0:
                    dve.drain()
                    for t in n:
                        nc.vector.bn_stats(stats[:, t, :], X[:, t, :])
                elif step == 1:
                    dve.drain()
                    for t in n:
                        nc.vector.bn_aggr(mv[:, t, :], stats[:, t, :])
                    dve.drain()
                    nc.vector.tensor_scalar(v, mv[:, ts, 1], eps, None, ALU.add)
                    dve.drain()
                    nc.vector.tensor_scalar(w.bitcast(I32), v.bitcast(I32), 1, None, ALU.arith_shift_right)
                    dve.drain()
                    nc.vector.tensor_scalar(r.bitcast(I32), w.bitcast(I32), -1.0, float(RSQRT_SEED), ALU.mult, ALU.add)
                    nc.vector.tensor_scalar(v, v, -0.5, None, ALU.mult)
                elif step < 4:
                    for _ in range(step - 1):
                        dve.drain()
                        nc.vector.tensor_tensor(w, r, r, ALU.mult)
                        dve.drain()
                        nc.vector.tensor_tensor(w, w, v, ALU.mult)
                        dve.drain()
                        nc.vector.scalar_tensor_tensor(out=r, in0=w, scalar=1.5, in1=r, op0=ALU.add, op1=ALU.mult)
                else:
                    dve.drain()
                    for t in n:
                        last = nc.vector.tensor_scalar(dst[:, t, :], X[:, t, :], mv[:, t, 0:1], rstd[:, t:t + 1],
                                                       ALU.subtract, ALU.mult)
                    if done:
                        last.then_inc(sem(done), 1)

            def layer_norm(dst, eps):
                for step in range(STEPS):
                    normalise(step, slice(0, NT), dst, eps)

            def outer_v(s):
                dve.wait_ge(sem("outer_in" + s), 16 * 8)
                dve.wait_ge(sem(s + "_v"), 1)
                for b in range(B):
                    last = nc.vector.tensor_tensor(vo[:, b, :], S_ps[1][:, b * P:(b + 1) * P], bv[s][:], ALU.add)
                last.then_inc(sem(s + "_v_sb"), 1)

            def token_softmax(s):
                outer_v(s)
                for b in range(B):
                    dve.wait_ge(sem(s + "_scores"), b + 1)
                    nc.vector.reduce_max(omax[0:M, b:b + 1], O_ps[b][0:M, :], AX)
                    dve.drain()
                    nc.vector.tensor_scalar(onmx[0:M, b:b + 1], omax[0:M, b:b + 1], -float(E) ** -0.5, None,
                                            ALU.mult).then_inc(sem(s + "_max"), 1)
                for b in range(B):
                    dve.wait_ge(sem(s + "_exp"), b + 1)
                    nc.vector.reciprocal(orec[0:M, b:b + 1], osum[0:M, b:b + 1])
                    dve.drain()
                    nc.vector.tensor_scalar(OP[0:M, b, :], OP[0:M, b, :], orec[0:M, b:b + 1], None, ALU.mult)\
                      .then_inc(sem(s + "_weights"), 1)
                for b in range(B):
                    dve.wait_ge(sem(s + "_pred"), b + 1)
                    rows = X[:, b * TB:(b + 1) * TB, :]
                    nc.vector.tensor_tensor(rows, tiles(W_ps[b][:]), rows, ALU.add)
                layer_norm(X, EPS_LATENT)
                dve.drain()
                for b in range(B):
                    rows = X[:, b * TB:(b + 1) * TB, :]
                    g = gam[s][:].unsqueeze(1).broadcast_to([P, TB, E])
                    nc.vector.tensor_tensor(rows, rows, g, ALU.mult)
                    dve.drain()
                    g = bet[s][:].unsqueeze(1).broadcast_to([P, TB, E])
                    nc.vector.tensor_tensor(rows, rows, g, ALU.add)\
                      .then_inc(sem("B_src" if s == "L0" else "out_ready"), 1)

            dve.wait_ge(sem("consts"), 1)
            dve.wait_ge(sem("ctx_sb"), 1)
            turned = S_ps[0][:, 0:B * P].rearrange("c (b m) -> c b m", b=B)
            for j in range(CBLK):
                cut = (j + 1) * M - CSTART[j]
                skip = M - cut
                end = CSTART[j + 1] - CSTART[j]
                nc.vector.tensor_copy(ctxV[0:CD, :, j, 0:cut], turned[0:CD, :, skip:M])
                last = nc.vector.tensor_copy(ctxV[CD:P, :, j, cut:end], turned[CD:P, :, 0:end - cut])
            last.then_inc(sem("ctx_sb"), 1)
            dve.wait_ge(sem("mask_in"), 32)
            nc.vector.tensor_scalar(self_bias[:], self_bias[:].bitcast(I32), 0, BIG, ALU.is_equal, ALU.mult)
            nc.vector.tensor_scalar(cross_bias[:], cmask_i[:], 0, BIG, ALU.is_equal, ALU.mult)
            dve.drain()
            nc.vector.tensor_reduce(bad[:, :, 0], self_bias[:, :, 0:KEYS], AX, ALU.min)
            nc.vector.tensor_reduce(bad[:, :, 1], self_bias[:, :, KEYS:T], AX, ALU.min)
            dve.drain()
            nc.vector.tensor_scalar(bad[:, :, 0], bad[:, :, 0], 0.0, None, ALU.is_equal)
            nc.vector.tensor_scalar(bad[:, :, 1], bad[:, :, 1], 0.0, None, ALU.is_gt)
            dve.drain()
            nc.vector.tensor_reduce(badp[:], bad[:].rearrange("p t a -> p (t a)"), AX, ALU.max)\
              .then_inc(sem("bad_rows"), 1)

            dve.wait_ge(sem("x_in"), 16)
            token_softmax("L0")
            outer_v("L1")
            for b in range(B):
                dve.wait_ge(sem("L1_scores"), b + 1)
                nc.vector.tensor_reduce(omax[:, b * TB:(b + 1) * TB], tiles(O_ps[b][:])[:, :, 0:M], AX, ALU.max)
                dve.drain()
                nc.vector.tensor_scalar(onmx[:, b * TB:(b + 1) * TB], omax[:, b * TB:(b + 1) * TB],
                                        -float(E) ** -0.5, None, ALU.mult).then_inc(sem("L1_max"), 1)
            for b in range(B):
                dve.wait_ge(sem("L1_exp"), b + 1)
                nc.vector.reciprocal(orec[:, b * TB:(b + 1) * TB], osum[:, b * TB:(b + 1) * TB])
                dve.drain()
                rows = XN[:, b * TB:(b + 1) * TB, 0:M]
                nc.vector.tensor_tensor(rows, rows, orec[:, b * TB:(b + 1) * TB].unsqueeze(2).broadcast_to([P, TB, M]),
                                        ALU.mult).then_inc(sem("L1_weights"), 1)
            nc.vector.tensor_tensor(X[:], X[:], bo1[:].unsqueeze(1).broadcast_to([P, NT, E]), ALU.add)
            dve.drain()
            for b in range(B):
                dve.wait_ge(sem("L1_out"), b + 1)
                rows = X[:, b * TB:(b + 1) * TB, :]
                nc.vector.tensor_tensor(rows, tiles(W_ps[b][:]), rows, ALU.add)
            dve.drain().then_inc(sem("L1_done"), 1)
            dve.wait_ge(sem("bad_sum"), 1)
            nc.vector.tensor_scalar(flag_f[:], O_ps[0][0:1, 0:1], 1.0, None, ALU.min)
            dve.drain()
            nc.vector.tensor_copy(flag[:], flag_f[:]).then_inc(sem("flag"), 1)

            def prepare(k, step, l):
                b = k % B
                ts = slice(b * TB, (b + 1) * TB)
                bias = (sob, cob, b2)[k // B]
                if step < STEPS:
                    normalise(step, ts, XN, EPS_DEC, "xn_ready")
                else:
                    if k == 2 * B:
                        dve.wait_ge(sem("ff_w"), 96 * l + 96)
                        nc.vector.memset(carrier[:, SLOTS + 1:SLOTS + 2], 0.0)
                    dve.drain()
                    nc.vector.tensor_tensor(X[:, ts, :], X[:, ts, :], bias[:].unsqueeze(1).broadcast_to([P, TB, E]),
                                            ALU.add)

            def work(ring, event, l, N, st=None):
                what, i = event
                if (ring.name, event) not in vector_empties:
                    return
                w = W_ps[ring.bank(event)]
                dve.wait_ge(sem(ring.full(event)), ring.value(event, l))
                if what == "n" and N is Nc:
                    nc.vector.tensor_copy(N[0:CD, i, :, :], tiles(w[0:CD, :])[:, 0:CBLK, :])
                    last = nc.vector.tensor_copy(N[CD:P, i, :, :], tiles(w[CD:P, :])[:, 1:TB, :])
                elif what == "V" and st.groups[i].cross:
                    last = nc.vector.tensor_copy(V[0:CW, i % 2, 0:CBLK, :], tiles(w[0:CW, 0:CBLK * P]))
                elif what == "n":
                    last = nc.vector.tensor_copy(N[:, i * TB:(i + 1) * TB, :], tiles(w[:]))
                elif what == "V":
                    last = nc.vector.tensor_copy(V[:, i % 2, :, :], tiles(w[:]))
                else:
                    i %= B
                    rows = X[:, i * TB:(i + 1) * TB, :]
                    last = nc.vector.tensor_tensor(rows, tiles(w[:]), rows, ALU.add)
                last.then_inc(sem(ring.free(event)), 1)

            def attention(st, l):
                C, ring = st.chunks, st.ring

                def masked(n):
                    group, qt = st.groups[n // TB], n % TB
                    b, s, w = group.b, n % SLOTS, group.keys
                    dve.wait_ge(sem(f"{st.name}_scores"), l * C + n + 1)
                    nc.vector.memset(carrier[:, s:s + 1], 0.0)
                    for t in range(group.heads):
                        cols = slice(t * w, (t + 1) * w)
                        row_bias = cross_bias[:, b, :] if group.cross else self_bias[:, b * TB + qt, group.key_base:T]
                        last = nc.vector.tensor_tensor_reduce(out=Sm[:, s, cols], in0=S_ps[n % len(S_ps)][:, cols], in1=row_bias,
                                                              scale=1.0, scalar=3.4e38, op0=ALU.add, op1=ALU.min,
                                                              accum_out=mn[:, s, t:t + 1])
                    last.then_inc(sem(f"{st.name}_masked"), 1)

                def reciprocals(n):
                    k = st.groups[n // TB].heads
                    dve.wait_ge(sem(f"{st.name}_exp"), l * C + n + 1)
                    nc.vector.reciprocal(rsum[:, n % SLOTS, 0:k], sums[:, n % SLOTS, 0:k]).then_inc(sem(f"{st.name}_rsum"), 1)

                for n in range(AHEAD):
                    masked(n)
                for n in range(C + TB + 2):
                    if n + AHEAD < C:
                        masked(n + AHEAD)
                    if n < C:
                        reciprocals(n)
                    if n > 1:
                        for event in st.plan[n - 2]:
                            work(ring, event, l, Nc, st)
                    for k, step in st.norm[n]:
                        prepare(k, step, l)

            dve.wait_ge(sem("pads_zero"), 1)
            dve.wait_ge(sem("flag"), 1)
            general = dve.value_load(flag[0:1, 0:1], min_val=0, max_val=1)
            with dve.Fori(0, L) as l:
                for step in range(STEPS):
                    prepare(0, step, l)
                dve.wait_ge(sem("self_w"), SELF_W * l + SELF_W)
                dve.wait_ge(sem("cross_w"), CROSS_W * l + CROSS_W)
                nc.vector.memset(carrier[:, SLOTS:SLOTS + 1], 0.0)
                prepare(0, STEPS, l)
                with dve.If(general > 0):
                    attention(STREAM_ALL, l)
                with dve.Else():
                    attention(STREAM_LAST, l)
                work(FFN, ("fin", 3), l, None)
                for step in range(STEPS + 1):
                    prepare(5, step, l)
                dve.drain()
                for b in range(B):
                    dve.wait_ge(sem("ff_out"), l * B + b + 1)
                    rows = X[:, b * TB:(b + 1) * TB, :]
                    last = nc.vector.tensor_tensor(rows, tiles(T_ps[b][:]), rows, ALU.add)
                last.then_inc(sem("ff_done"), 1)
            dve.drain().then_inc(sem("C_src"), 2)
            token_softmax("L3")


_OUT_SHAPE = (2, 512, 128)


def kernel(**inputs):
    import numpy as _np
    import concourse.bacc as _bacc
    from concourse import mybir as _mybir
    from concourse.bass_utils import run_bass_kernel_spmd as _run

    nc = _bacc.Bacc("TRN2", target_bir_lowering=False, num_devices=1)
    arrays, args = {}, {}
    for name, value in inputs.items():
        v = _np.ascontiguousarray(value)
        arrays[f"in_{name}"] = v
        args[name] = nc.dram_tensor(f"in_{name}", v.shape, _mybir.dt.from_np(v.dtype), kind="ExternalInput").ap()
    out = nc.dram_tensor("out_x", _OUT_SHAPE, _mybir.dt.float32, kind="ExternalOutput").ap()
    build(nc, args, out)
    r = _run(nc, [arrays], core_ids=[0])
    return r.results[0]["out_x"]
```
